# Optimizing a Trainium2 kernel written in Bass

```python
import numpy as np
import jax
import jax.numpy as jnp

def _softmax(x, axis=-1):
    return jax.nn.softmax(x, axis=axis)

def _gelu(x):
    return jax.nn.gelu(x, approximate=True)

def _silu(x):
    return jax.nn.silu(x)

def _sigmoid(x):
    return jax.nn.sigmoid(x)

def _layernorm(x, axis=-1, eps=1e-05):
    m = jnp.mean(x, axis=axis, keepdims=True)
    v = jnp.var(x, axis=axis, keepdims=True)
    return (x - m) / jnp.sqrt(v + eps)

def _scatter_add(tgt, idx, src, axis=0):
    return tgt.at[idx].add(src)

def _segment_sum(src, seg, n):
    return jax.ops.segment_sum(src, seg, n)
kernel_name = 'mk_cond_resid_d1_seqx_r4_46257e'

def setup_inputs(seed: int=0):
    np.random.seed(seed)
    _w = jnp.asarray

    def _rec_inputs():
        import jax
        import jax.numpy as jnp
        _rk = jax.random.key(seed)
        x = 7.22e-05 + 1 * jax.random.normal(jax.random.fold_in(_rk, 1), (8, 256, 256), jnp.float32)
        _lenS = 256 - jax.random.randint(jax.random.fold_in(_rk, 7), (8,), 0, max(1, 256 // 4) + 1, jnp.int32)
        _lenS2 = 256 - jax.random.randint(jax.random.fold_in(_rk, 8), (8,), 0, max(1, 256 // 4) + 1, jnp.int32)
        cond_256 = 0.000887014 + 1.03683 * jax.random.normal(jax.random.fold_in(_rk, 11), (8, 64), jnp.float32)
        return (x, cond_256)
    x, cond_256 = _rec_inputs()

    def _L0_cond_setup():
        import jax, jax.numpy as jnp
        import numpy as np
        D_MODEL = 256
        D_T = 64
        N_HEADS = 16
        HIDDEN = 4 * D_MODEL
        EPS = 1e-06

        def _tc_rmsnorm(x, t, gw, gb, bw, bb):
            g = (t @ gw.T + gb)[:, None, :]
            b = (t @ bw.T + bb)[:, None, :]
            inv_rms = jax.lax.rsqrt(jnp.mean(x * x, axis=-1, keepdims=True) + EPS)
            return g * x * inv_rms + b

        def _attention(x, Wq, Wk, Wv, Wo):
            B, L, D = x.shape
            H = N_HEADS
            dh = D // H
            scale = np.sqrt(dh).astype(np.float32)
            q = (x @ Wq.T).reshape(B, L, H, dh)
            k = (x @ Wk.T).reshape(B, L, H, dh)
            v = (x @ Wv.T).reshape(B, L, H, dh)
            attn = jnp.einsum('blhd,bmhd->bhlm', q, k) / scale
            p = jax.nn.softmax(attn, axis=-1)
            o = jnp.einsum('bhlm,bmhd->blhd', p, v).reshape(B, L, D)
            return o @ Wo.T

        def _swiglu(x, gate_w, hid_w, out_w):
            return jax.nn.silu(x @ gate_w.T) * (x @ hid_w.T) @ out_w.T
        key = jax.random.key(seed)
        ks = jax.random.split(key, 20)
        B, L = (8, 256)
        s_d = 1.0 / np.sqrt(D_MODEL)
        s_t = 1.0 / np.sqrt(D_T)
        s_h = 1.0 / np.sqrt(HIDDEN)
        return {'x': jax.random.normal(ks[0], (B, L, D_MODEL), jnp.float32), 't': jax.random.normal(ks[1], (B, D_T), jnp.float32), 'Wq': jax.random.normal(ks[2], (D_MODEL, D_MODEL), jnp.float32) * s_d, 'Wk': jax.random.normal(ks[3], (D_MODEL, D_MODEL), jnp.float32) * s_d, 'Wv': jax.random.normal(ks[4], (D_MODEL, D_MODEL), jnp.float32) * s_d, 'Wo': jax.random.normal(ks[5], (D_MODEL, D_MODEL), jnp.float32) * s_d, 'g1w': jax.random.normal(ks[6], (D_MODEL, D_T), jnp.float32) * s_t, 'g1b': jnp.ones((D_MODEL,), jnp.float32), 'b1w': jax.random.normal(ks[7], (D_MODEL, D_T), jnp.float32) * s_t, 'b1b': jnp.zeros((D_MODEL,), jnp.float32), 'g2w': jax.random.normal(ks[8], (D_MODEL, D_T), jnp.float32) * s_t, 'g2b': jnp.ones((D_MODEL,), jnp.float32), 'b2w': jax.random.normal(ks[9], (D_MODEL, D_T), jnp.float32) * s_t, 'b2b': jnp.zeros((D_MODEL,), jnp.float32), 'gate_w': jax.random.normal(ks[10], (HIDDEN, D_MODEL), jnp.float32) * s_d, 'hid_w': jax.random.normal(ks[11], (HIDDEN, D_MODEL), jnp.float32) * s_d, 'out_w': jax.random.normal(ks[12], (D_MODEL, HIDDEN), jnp.float32) * s_h}
    _L0_cond_all = _L0_cond_setup()
    _L0_cond_in = {k: v for k, v in _L0_cond_all.items() if k in ('Wq', 'Wk', 'Wv', 'Wo', 'g1w', 'g1b', 'b1w', 'b1b', 'g2w', 'g2b', 'b2w', 'b2b', 'gate_w', 'hid_w', 'out_w')}
    del _L0_cond_all
    return {'x': x, 'cond_256': cond_256, 'L0_cond_Wq': _L0_cond_in['Wq'], 'L0_cond_Wk': _L0_cond_in['Wk'], 'L0_cond_Wv': _L0_cond_in['Wv'], 'L0_cond_Wo': _L0_cond_in['Wo'], 'L0_cond_g1w': _L0_cond_in['g1w'], 'L0_cond_g1b': _L0_cond_in['g1b'], 'L0_cond_b1w': _L0_cond_in['b1w'], 'L0_cond_b1b': _L0_cond_in['b1b'], 'L0_cond_g2w': _L0_cond_in['g2w'], 'L0_cond_g2b': _L0_cond_in['g2b'], 'L0_cond_b2w': _L0_cond_in['b2w'], 'L0_cond_b2b': _L0_cond_in['b2b'], 'L0_cond_gate_w': _L0_cond_in['gate_w'], 'L0_cond_hid_w': _L0_cond_in['hid_w'], 'L0_cond_out_w': _L0_cond_in['out_w']}

def reference(x, cond_256, L0_cond_Wq, L0_cond_Wk, L0_cond_Wv, L0_cond_Wo, L0_cond_g1w, L0_cond_g1b, L0_cond_b1w, L0_cond_b1b, L0_cond_g2w, L0_cond_g2b, L0_cond_b2w, L0_cond_b2b, L0_cond_gate_w, L0_cond_hid_w, L0_cond_out_w):
    import jax
    import jax.numpy as jnp

    def _L0_cond_ref(x, t, Wq, Wk, Wv, Wo, g1w, g1b, b1w, b1b, g2w, g2b, b2w, b2b, gate_w, hid_w, out_w):
        import jax, jax.numpy as jnp
        import numpy as np
        D_MODEL = 256
        D_T = 64
        N_HEADS = 16
        HIDDEN = 4 * D_MODEL
        EPS = 1e-06

        def _tc_rmsnorm(x, t, gw, gb, bw, bb):
            g = (t @ gw.T + gb)[:, None, :]
            b = (t @ bw.T + bb)[:, None, :]
            inv_rms = jax.lax.rsqrt(jnp.mean(x * x, axis=-1, keepdims=True) + EPS)
            return g * x * inv_rms + b

        def _attention(x, Wq, Wk, Wv, Wo):
            B, L, D = x.shape
            H = N_HEADS
            dh = D // H
            scale = np.sqrt(dh).astype(np.float32)
            q = (x @ Wq.T).reshape(B, L, H, dh)
            k = (x @ Wk.T).reshape(B, L, H, dh)
            v = (x @ Wv.T).reshape(B, L, H, dh)
            attn = jnp.einsum('blhd,bmhd->bhlm', q, k) / scale
            p = jax.nn.softmax(attn, axis=-1)
            o = jnp.einsum('bhlm,bmhd->blhd', p, v).reshape(B, L, D)
            return o @ Wo.T

        def _swiglu(x, gate_w, hid_w, out_w):
            return jax.nn.silu(x @ gate_w.T) * (x @ hid_w.T) @ out_w.T
        x = x + _attention(_tc_rmsnorm(x, t, g1w, g1b, b1w, b1b), Wq, Wk, Wv, Wo)
        return x + _swiglu(_tc_rmsnorm(x, t, g2w, g2b, b2w, b2b), gate_w, hid_w, out_w)
    x = x + _L0_cond_ref(x, cond_256, L0_cond_Wq, L0_cond_Wk, L0_cond_Wv, L0_cond_Wo, L0_cond_g1w, L0_cond_g1b, L0_cond_b1w, L0_cond_b1b, L0_cond_g2w, L0_cond_g2b, L0_cond_b2w, L0_cond_b2b, L0_cond_gate_w, L0_cond_hid_w, L0_cond_out_w)
    return x

_drawn_inputs = setup_inputs


def setup_inputs(seed=0):
    import zlib

    import numpy as np

    out = dict(_drawn_inputs(seed))
    spreads = {'L0_cond_g1b': (1.0, 0.2),
     'L0_cond_b1b': (0.0, 0.1),
     'L0_cond_g2b': (1.0, 0.2),
     'L0_cond_b2b': (0.0, 0.1)}
    factors = {}
    for name, (base, spread) in spreads.items():
        noise = np.random.default_rng([zlib.crc32(name.encode()), seed]).standard_normal(out[name].shape)
        drawn = base * np.exp(spread * noise) if base else spread * noise
        out[name] = jnp.asarray(drawn.astype(out[name].dtype))
    for name, factor in factors.items():
        out[name] = (out[name] * factor).astype(out[name].dtype)
    return out
```

```python
from contextlib import ExitStack

import concourse.bass as bass
from concourse import mybir

F32 = mybir.dt.float32
F32R = mybir.dt.float32r
I32 = mybir.dt.int32
ALU = mybir.AluOpType
ACT = mybir.ActivationFunctionType
AX = mybir.AxisListType

P = 128
B, T, D = 8, 256, 256
HEADS, DH = 16, 16
HIDDEN = 1024
DT = 64
KT = D // P
TT = T // P
HT = HIDDEN // P
SLOTS = HEADS // 2
GROUPS = 4
CHUNKS = 8
EPS = 1e-6
QSCALE = 1.0 / 4.0
LOOP_FROM, LOOP_TO = 2, 6
STACK_DMAS = 7
RSQRT_MAGIC = float(0x5F3759DF)

F1A, STAT1, F1B, F1C, F1D, VV, F1E, WO, QQ, KK, STAT2, F1F, F1G, F1H, MT, F2 = range(16)
UP_UNITS = (F1A, F1B, F1C, F1D, F1E, F1F, F1G, F1H)
FILLS = 5
NEWTONS = 3
NEWTON_STEPS = 3 + 4 * NEWTONS


class Step:

    def __init__(self, i, parity, looped):
        self.i, self.parity, self.looped = i, parity, looped
        inside = (lambda b: True) if looped else (lambda b: 0 <= b < B)
        self.a = i + 2 if inside(i + 2) else None
        self.s = i + 1 if inside(i + 1) else None
        self.c = i if inside(i) else None
        self.n = i - 1 if inside(i - 1) else None
        self.f = i - 2 if inside(i - 2) else None
        self.first = not looped and i == -2

    def at(self, i):
        return not self.looped and self.i == i


def steps(engine, emit):
    for i in range(-2, LOOP_FROM):
        emit(Step(i, i % 2, False))
    with engine.Fori(LOOP_FROM // 2, LOOP_TO // 2) as pair:
        for u in range(2):
            emit(Step(pair * 2 + u, u, True))
    for i in range(LOOP_TO, B + 2):
        emit(Step(i, i % 2, False))


F_START = 1
STORE_START = 16


def layer_kernel(nc, x_t, cond_t, cond_w, cond_b, w_attn, w_gate, w_hid, w_out, consts, score_rows, out_t):
    ctx = ExitStack()
    with ctx:
        def sb(name, shape, dt=F32):
            return ctx.enter_context(nc.sbuf_tensor(name, shape, dt))

        def pb(name, shape):
            return ctx.enter_context(nc.psum_tensor(name, shape, F32))

        def sem(name):
            return ctx.enter_context(nc.semaphore(name))

        x_sb = sb("x_sb", [P, KT, B * T])
        ct_sb = sb("ct_sb", [DT, B])
        cb_sb = sb("cb_sb", [P, 4 * KT])
        const_sb = sb("const_sb", [P, P + 2])
        ident, rows_lo, rows_hi = const_sb[:, 0:P], const_sb[:, P:P + 1], const_sb[:, P + 1:P + 2]
        mean_w = sb("mean_w", [P, P])
        three_halves = sb("three_halves", [P, T // 32])
        zero_rows = sb("zero_rows", [32, T])
        gb = sb("gb", [P, 4 * KT, B])
        raw = [sb(f"raw{n}", [P, 2048]) for n in range(3)]
        attn_hi, attn_lo = sb("attn_hi", [P, KT, 4 * D], F32R), sb("attn_lo", [P, KT, 4 * D], F32R)
        gate_hi, gate_lo = sb("gate_hi", [P, KT, HIDDEN], F32R), sb("gate_lo", [P, KT, HIDDEN], F32R)
        hid_hi, hid_lo = sb("hid_hi", [P, KT, HIDDEN], F32R), sb("hid_lo", [P, KT, HIDDEN], F32R)
        out_hi, out_lo = sb("out_hi", [P, HT, D], F32R), sb("out_lo", [P, HT, D], F32R)

        norm_sum = [sb(f"norm_sum{n}", [P, T]) for n in range(2)]
        norm_tr = [sb(f"norm_tr{n}", [P, T // 32, 32]) for n in range(2)]
        newton = [sb(f"newton{n}", [P, 4, T // 32]) for n in range(2)]
        norm_inv = sb("norm_inv", [P, T])
        norm_x = [sb(f"norm_x{n}", [P, KT, T]) for n in range(2)]
        norm_sq = norm_y = norm_x
        h_hi, h_lo = sb("h_hi", [P, 2, KT, T], F32R), sb("h_lo", [P, 2, KT, T], F32R)
        g_hi, g_lo = sb("g_hi", [P, KT, T], F32R), sb("g_lo", [P, KT, T], F32R)
        qk = sb("qk", [P, KT, 4, T], F32R)
        Q_HI, Q_LO, K_HI, K_LO = range(4)
        stack = [sb(f"stack{n}", [P, SLOTS, 2, T], F32R) for n in range(2)]
        v_aug = [sb(f"v_aug{n}", [P, TT, 2, SLOTS, 32]) for n in range(2)]
        m_raw = sb("m_raw", [P, TT, 2, SLOTS])
        m_split = sb("m_split", [P, TT, 2, 2, SLOTS], F32R)
        m_rows = sb("m_rows", [32, T])
        probs = sb("probs", [P, 2, 2, 2, T])
        on_hi, on_lo = sb("on_hi", [P, 2, T], F32R), sb("on_lo", [P, 2, T], F32R)
        s_pack = sb("s_pack", [P, 2, T])
        o_norm = s_pack
        act_hi, act_lo = sb("act_hi", [P, HT, T], F32R), sb("act_lo", [P, HT, T], F32R)
        cw_sb = probs[0:DT, 0, :, :, :].rearrange("p a b n -> p (a b) n")

        def place(n, k, tiles):
            return raw[n][:, k * T:(k + tiles) * T].rearrange("p (a t) -> p a t", t=T)

        act_f, s_bcast, x1 = place(0, 0, 4), place(0, 4, 2), place(0, 6, 2)
        resid = raw[1][:, 0:4 * T].rearrange("p (b a t) -> p b a t", b=2, t=T)
        y_sb, o_pack = place(1, 4, 2), place(1, 6, 2)
        th, o_part, s_part = place(2, 0, 2), place(2, 2, 2), place(2, 4, 2)
        s_recip = s_part

        s_ps = pb("s_ps", [P, 2, 2, T])
        st_ps = pb("st_ps", [P, 2, 2, T])
        o_ps = pb("o_ps", [P, 2, 2, T])
        dense = [pb(f"dense{n}", [P, 2, T]) for n in range(2)]

        x_loaded = [sem(f"x_loaded{n}") for n in range(3)]
        cond_loaded, const_loaded, score_rows_loaded = sem("cond_loaded"), sem("const_loaded"), sem("score_rows_loaded")
        score_rows_staged = sem("score_rows_staged")
        w_loaded = [sem(f"w_loaded{n}") for n in range(4)]
        w_hi_done = [sem(f"w_hi_done{n}") for n in range(4)]
        w_lo_done = [sem(f"w_lo_done{n}") for n in range(4)]
        filled, gb_product, gb_ready = sem("filled"), sem("gb_product"), sem("gb_ready")
        squares = [sem(f"squares{n}") for n in range(2)]
        square_sums = [sem(f"square_sums{n}") for n in range(2)]
        stats_done = [sem(f"stats_done{n}") for n in range(2)]
        stats_turned = [sem(f"stats_turned{n}") for n in range(2)]
        newton_step = [sem(f"newton_step{n}") for n in range(2)]
        inv_spread = [sem(f"inv_spread{n}") for n in range(2)]
        x_scaled = [sem(f"x_scaled{n}") for n in range(2)]
        norm_ready = [sem(f"norm_ready{n}") for n in range(2)]
        norm_hi = [sem(f"norm_hi{n}") for n in range(2)]
        norm_lo = [sem(f"norm_lo{n}") for n in range(2)]
        q_done, k_done, v_done = sem("q_done"), sem("k_done"), sem("v_done")
        qk_hi_ready, qk_lo_ready, v_ready = sem("qk_hi_ready"), sem("qk_lo_ready"), sem("v_ready")
        stack_loaded = [sem(f"stack_loaded{n}") for n in range(GROUPS)]
        scores_done, maxed, m_hi_ready, m_split_ready = sem("scores_done"), sem("maxed"), sem("m_hi_ready"), sem("m_split_ready")
        m_turned, m_rows_ready, m_loaded = sem("m_turned"), sem("m_rows_ready"), sem("m_loaded")
        scores_t_done, exp_done, pv_done = sem("scores_t_done"), sem("exp_done"), sem("pv_done")
        o_parts_ready, o_packed, s_spread, s_inverted, o_normed = (
            sem("o_parts_ready"), sem("o_packed"), sem("s_spread"), sem("s_inverted"), sem("o_normed"))
        on_hi_ready, on_lo_ready = sem("on_hi_ready"), sem("on_lo_ready")
        wo_done, x1_ready, resid_ready = sem("wo_done"), sem("x1_ready"), sem("resid_ready")
        f1_done, tanh_ready, silu_ready, act_ready = sem("f1_done"), sem("tanh_ready"), sem("silu_ready"), sem("act_ready")
        act_hi_ready, act_lo_ready, f2_done, y_ready, y_stored = (
            sem("act_hi_ready"), sem("act_lo_ready"), sem("f2_done"), sem("y_ready"), sem("y_stored"))

        ATTN, GATE, HID, OUT = range(4)
        w_raw = [raw[0], raw[1], raw[2], raw[0]]
        w_hi_sb = [attn_hi, gate_hi, hid_hi, out_hi]
        w_lo_sb = [attn_lo, gate_lo, hid_lo, out_lo]

        def raw_view(w):
            return w_raw[w][:, :].rearrange("p (a n) -> p a n", a=w_hi_sb[w].shape[1])

        def tokens(b):
            return bass.ds(b * T, T)

        def norm_buffer_free(engine, st, n):
            if n == 0 and (st.looped or st.a >= 2):
                engine.wait_ge(v_done, st.a - 1)
            if n == 1:
                engine.wait_ge(f1_done, HT * st.n)

        block = ctx.enter_context(nc.Block())

        @block.sync
        def _(sp):
            def load_x(n, lo, hi):
                sp.dma_start(x_sb[:, :, lo * T:hi * T], x_t[:, :, lo * T:hi * T]).then_inc(x_loaded[n], 16)

            load_x(0, 0, 1)
            for counts in (act_ready, act_hi_ready, act_lo_ready, y_ready):
                sp.sem_inc(counts, F_START)
            sp.sem_inc(y_stored, STORE_START)
            sp.dma_start(raw[0][:, :], w_attn).then_inc(w_loaded[ATTN], 16)
            load_x(1, 1, 4)
            sp.dma_start(raw[1][:, :], w_gate).then_inc(w_loaded[GATE], 16)
            load_x(2, 4, B)
            staged = raw[2][0:32, :].rearrange("p (s t) -> p s t", t=T)
            sp.dma_start(staged, score_rows).then_inc(score_rows_staged, 16)
            sp.wait_ge(score_rows_staged, 16)
            for n in range(2):
                sp.dma_start(stack[n][3:P:4, :, 1, :].bitcast(F32), staged).then_inc(score_rows_loaded, 16)
            sp.wait_ge(score_rows_loaded, 32)
            sp.dma_start(raw[2][:, :], w_hid).then_inc(w_loaded[HID], 16)

            def stack_group(st, g):
                if st.c is not None:
                    sp.wait_ge(scores_t_done, CHUNKS * st.c + 2 * g + 2)
                if st.first and g == 0:
                    sp.wait_ge(filled, FILLS)
                if g == 0:
                    sp.wait_ge(qk_lo_ready, 2 * (st.a + 1))
                dst = stack[st.parity]
                sp.dma_start(dst[3:P:4, 2 * g:2 * g + 2, 0, :].bitcast(F32), zero_rows[:, :].unsqueeze(1).broadcast_to([32, 2, T])).then_inc(stack_loaded[g], 16)
                for sl in range(2):
                    slot = 2 * g + sl
                    j = slot % 4
                    src = qk[32 * j:32 * j + 32, slot // 4, :, :].bitcast(F32)
                    for r, pair in enumerate((src[:, Q_HI:K_HI + 1:2, :], src[:, Q_LO:K_HI + 1, :], src[:, Q_HI:K_LO + 1:3, :])):
                        sp.dma_start(dst[r:P:4, slot, :, :].bitcast(F32), pair).then_inc(stack_loaded[g], 16)

            def emit(st):
                if st.a is not None:
                    stack_group(st, 0)
                    stack_group(st, 1)
                if st.s is not None:
                    sp.wait_ge(m_rows_ready, st.s + 1)
                    sp.dma_start(stack[1 - st.parity][3:P:4, :, 0, :].bitcast(F32),
                                 m_rows[:, :].unsqueeze(1).broadcast_to([32, SLOTS, T])).then_inc(m_loaded, 16)
                if st.first:
                    sp.wait_ge(w_lo_done[ATTN], 1)
                    sp.dma_start(raw[0][:, :], w_out).then_inc(w_loaded[OUT], 16)
                if st.a is not None:
                    stack_group(st, 2)
                    stack_group(st, 3)
                if st.f is not None:
                    sp.wait_ge(y_ready, F_START + st.f + 1)
                    sp.dma_start(out_t[:, :, tokens(st.f)], y_sb).then_inc(y_stored, 16)

            steps(sp, emit)
            sp.wait_ge(y_stored, STORE_START + 16 * B)

        @block.tensor
        def _(pe):
            read_signal = {STAT1: (2, stats_turned[0], 1, 1), QQ: (2, qk_lo_ready, 2, 1), KK: (2, qk_lo_ready, 2, 2),
                           VV: (1, v_ready, 2, 2), MT: (1, m_rows_ready, 1, 1), WO: (-1, x1_ready, 1, 1),
                           STAT2: (-1, stats_turned[1], 1, 1), F2: (-2, y_ready, 1, F_START + 1)}
            read_signal |= {unit: (-2, act_ready, HT, F_START + m + 1) for m, unit in enumerate(UP_UNITS)}

            def dense_bank(st, unit):
                i, before = st.i, unit - 2
                while True:
                    if before < 0:
                        i, before = i - 1, before + len(read_signal)
                    ahead, signal, per_batch, within = read_signal[before]
                    batch = i + ahead
                    if st.looped or 0 <= batch < B:
                        pe.wait_ge(signal, per_batch * batch + within)
                        break
                    if i < -2:
                        break
                    before -= 2
                return dense[unit % 2]

            def product(out, passes):
                for n, (w, m) in enumerate(passes):
                    last = nc.tensor.matmul(out, w, m, start=(n == 0), stop=(n == len(passes) - 1))
                return last

            def three(w_hi, w_lo, m_hi, m_lo, ks):
                return [pair for k in ks for pair in ((w_hi(k), m_hi(k)), (w_hi(k), m_lo(k)), (w_lo(k), m_hi(k)))]

            def columns(w, first):
                return lambda k: w[:, k, first:first + P]

            def stats(st, n, b):
                d = dense_bank(st, STAT1 if n == 0 else STAT2)
                pe.wait_ge(square_sums[n], b + 1)
                product(d[:, 0, :], [(mean_w[:, :], norm_sum[n][:, :])]).then_inc(stats_done[n], 1)

            def project(st, unit, first_col, done):
                d = dense_bank(st, unit)
                h = st.parity
                for m in range(KT):
                    last = product(d[:, m, :], three(columns(attn_hi, first_col + m * P), columns(attn_lo, first_col + m * P),
                                                     lambda k: h_hi[:, h, k, :], lambda k: h_lo[:, h, k, :], range(KT)))
                last.then_inc(done, 1)

            def values(st):
                d = dense_bank(st, VV)
                h = 1 - st.parity
                for t in range(TT):
                    tok = slice(t * P, t * P + P)
                    last = product(d[:, t, :], three(lambda k: h_hi[:, h, k, tok], lambda k: h_lo[:, h, k, tok],
                                                     lambda k: attn_hi[:, k, 2 * D:3 * D], lambda k: attn_lo[:, k, 2 * D:3 * D],
                                                     range(KT)))
                last.then_inc(v_done, 1)

            def scores(st, chunk):
                g, half = chunk // 2, chunk % 2
                if half == 0:
                    pe.wait_ge(stack_loaded[g], 16 * STACK_DMAS * (st.s + 1))
                pe.wait_ge(maxed, CHUNKS * st.s + chunk)
                buf = stack[1 - st.parity]
                for sl in range(2):
                    for par in range(2):
                        win = slice(64 * par, 64 * par + 64)
                        last = product(s_ps[:, par, sl, :], [(buf[win, 2 * g + sl, 0, half * P:half * P + P],
                                                              buf[win, 2 * g + sl, 1, :])])
                last.then_inc(scores_done, 1)

            def scores_t(st, chunk):
                g, half = chunk // 2, chunk % 2
                if chunk == 0:
                    pe.wait_ge(m_loaded, 16 * (st.c + 1))
                pe.wait_ge(exp_done, CHUNKS * st.c + chunk)
                buf = stack[st.parity]
                for sl in range(2):
                    for par in range(2):
                        win = slice(64 * par, 64 * par + 64)
                        last = product(st_ps[:, par, sl, :], [(buf[win, 2 * g + sl, 1, half * P:half * P + P],
                                                               buf[win, 2 * g + sl, 0, :])])
                last.then_inc(scores_t_done, 1)

            def probs_v(st, chunk):
                g, half = chunk // 2, chunk % 2
                if chunk == 0:
                    pe.wait_ge(v_ready, 2 * (st.c + 1))
                    pe.wait_ge(o_packed, 2 * st.c)
                pe.wait_ge(exp_done, CHUNKS * st.c + chunk + 1)
                for j in range(4):
                    last = nc.tensor.matmul(o_ps[32 * j:32 * j + 32, g // 2, g % 2, :],
                                            v_aug[st.parity][:, half, g % 2, 4 * (g // 2) + j, :],
                                            probs[:, chunk % 2, j % 2, j // 2, :], start=(half == 0), stop=(half == 1))
                last.then_inc(pv_done, 1)

            def max_rows(st):
                d = dense_bank(st, MT)
                pe.wait_ge(m_split_ready, st.s + 1)
                for t in range(TT):
                    lhs = m_split[:, t, :, :, :].rearrange("p a b s -> p (a b s)").bitcast(F32)
                    last = product(d[0:32, 0, t * P:t * P + P], [(lhs, ident)])
                last.then_inc(m_turned, 1)

            def out_proj(st):
                d = dense_bank(st, WO)
                pe.wait_ge(on_hi_ready, st.n + 1)
                pe.wait_ge(on_lo_ready, st.n + 1)
                for m in range(KT):
                    last = product(d[:, m, :], three(columns(attn_hi, 3 * D + m * P), columns(attn_lo, 3 * D + m * P),
                                                     lambda k: on_hi[:, k, :], lambda k: on_lo[:, k, :], range(2)))
                last.then_inc(wo_done, 1)

            def ffn_up(st, m, unit):
                d = dense_bank(st, unit)
                if m == 0:
                    pe.wait_ge(norm_hi[1], st.f + 1)
                    pe.wait_ge(norm_lo[1], st.f + 1)
                for half, (hi, lo) in enumerate(((gate_hi, gate_lo), (hid_hi, hid_lo))):
                    last = product(d[:, half, :], three(columns(hi, m * P), columns(lo, m * P),
                                                        lambda k: g_hi[:, k, :], lambda k: g_lo[:, k, :], range(KT)))
                last.then_inc(f1_done, 1)

            down = {}

            def ffn_down(st, part):
                if part == 0:
                    down["bank"] = dense_bank(st, F2)
                if part < 2:
                    pe.wait_ge(act_hi_ready, F_START + HT * st.f + 4 * (part + 1))
                    pe.wait_ge(act_lo_ready, F_START + HT * st.f + 4 * (part + 1))
                m, ks = part // 2, range(4 * (part % 2), 4 * (part % 2) + 4)
                passes = three(columns(out_hi, m * P), columns(out_lo, m * P),
                               lambda k: act_hi[:, k, :], lambda k: act_lo[:, k, :], ks)
                for n, (w, mov) in enumerate(passes):
                    last = nc.tensor.matmul(down["bank"][:, m, :], w, mov, start=(part % 2 == 0 and n == 0),
                                            stop=(part % 2 == 1 and n == len(passes) - 1))
                if part == 3:
                    last.then_inc(f2_done, 1)

            pe.wait_ge(cond_loaded, 16 * 3)
            for n in range(4 * KT):
                last = product(s_ps[:, 0, 0, n * B:n * B + B], [(cw_sb[:, n // KT, (n % KT) * P:(n % KT) * P + P], ct_sb[:, :])])
            last.then_inc(gb_product, 1)
            pe.wait_ge(filled, FILLS)
            pe.wait_ge(const_loaded, 16)

            def emit(st):
                A, S, C, N, F = (b is not None for b in (st.a, st.s, st.c, st.n, st.f))
                if st.at(1):
                    for w in (GATE, HID, OUT):
                        pe.wait_ge(w_lo_done[w], 1)
                if S:
                    if st.at(-1):
                        pe.wait_ge(gb_ready, 1)
                        pe.wait_ge(score_rows_loaded, 32)
                    scores(st, 0)
                if F:
                    ffn_up(st, 0, F1A)
                if C:
                    scores_t(st, 0)
                if A:
                    stats(st, 0, st.a)
                if F:
                    ffn_up(st, 1, F1B)
                if C:
                    probs_v(st, 0)
                if S:
                    scores(st, 1)
                if C:
                    scores_t(st, 1)
                if F:
                    ffn_up(st, 2, F1C)
                if C:
                    probs_v(st, 1)
                if F:
                    ffn_up(st, 3, F1D)
                if S:
                    scores(st, 2)
                if C:
                    scores_t(st, 2)
                if S:
                    values(st)
                    scores(st, 3)
                if C:
                    probs_v(st, 2)
                if F:
                    ffn_up(st, 4, F1E)
                if C:
                    scores_t(st, 3)
                if N:
                    out_proj(st)
                if S:
                    scores(st, 4)
                if C:
                    probs_v(st, 3)
                if A:
                    if st.first:
                        pe.wait_ge(w_hi_done[ATTN], 1)
                        pe.wait_ge(w_lo_done[ATTN], 1)
                    pe.wait_ge(norm_hi[0], st.a + 1)
                    pe.wait_ge(norm_lo[0], st.a + 1)
                    project(st, QQ, 0, q_done)
                if C:
                    scores_t(st, 4)
                if A:
                    project(st, KK, D, k_done)
                if S:
                    scores(st, 5)
                if C:
                    probs_v(st, 4)
                if N:
                    stats(st, 1, st.n)
                if F:
                    ffn_up(st, 5, F1F)
                if C:
                    scores_t(st, 5)
                if F:
                    ffn_up(st, 6, F1G)
                if S:
                    scores(st, 6)
                if C:
                    probs_v(st, 5)
                if F:
                    ffn_up(st, 7, F1H)
                if C:
                    scores_t(st, 6)
                if F:
                    ffn_down(st, 0)
                if S:
                    scores(st, 7)
                if C:
                    probs_v(st, 6)
                if F:
                    ffn_down(st, 1)
                if C:
                    scores_t(st, 7)
                if F:
                    ffn_down(st, 2)
                if S:
                    max_rows(st)
                if C:
                    probs_v(st, 7)
                if F:
                    ffn_down(st, 3)

            steps(pe, emit)

        @block.scalar
        def _(act):
            act.dma_start(ct_sb[:, :], cond_t).then_inc(cond_loaded, 16)
            act.dma_start(cw_sb[:, :, :], cond_w).then_inc(cond_loaded, 16)
            act.dma_start(cb_sb[:, :], cond_b).then_inc(cond_loaded, 16)
            act.dma_start(const_sb[:, :], consts).then_inc(const_loaded, 16)

            def split_hi(w):
                act.wait_ge(w_loaded[w], 16)
                nc.scalar.activation(w_hi_sb[w][:, :, :], raw_view(w), ACT.Copy).then_inc(w_hi_done[w], 1)

            def norm_round(st, n, b):
                dst = h_hi[:, st.parity, :, :] if n == 0 else g_hi[:, :, :]
                act.wait_ge(norm_ready[n], 2 * (b + 1))
                norm_buffer_free(act, st, n)
                nc.scalar.activation(dst, norm_y[n][:, :, :], ACT.Copy).then_inc(norm_hi[n], 1)

            def exps(st, chunk):
                act.wait_ge(scores_t_done, CHUNKS * st.c + chunk + 1)
                if chunk >= 2 or st.looped or st.c > 0:
                    act.wait_ge(pv_done, CHUNKS * st.c + chunk - 1)
                nc.scalar.activation(probs[:, chunk % 2, :, :, :], st_ps[:, :, :, :], ACT.Exp).then_inc(exp_done, 1)

            def tanh(st, m):
                act.wait_ge(f1_done, HT * st.f + m + 1)
                act.wait_ge(act_ready, F_START + HT * st.f + max(m - 1, 0))
                bank = dense[UP_UNITS[m] % 2]
                nc.scalar.activation(th[:, m % 2, :], bank[:, 0, :], ACT.Tanh, scale=0.5).then_inc(tanh_ready, 1)

            def act_round(st, m):
                act.wait_ge(act_ready, F_START + HT * st.f + m + 1)
                nc.scalar.activation(act_hi[:, m, :], act_f[:, m % 4, :], ACT.Copy).then_inc(act_hi_ready, 1)

            def o_parts(st):
                act.wait_ge(pv_done, CHUNKS * (st.n + 1))
                act.wait_ge(o_normed, 2 * st.n)
                nc.scalar.activation(o_part[:, :, :], o_ps[:, :, 0, :], ACT.Identity, scale=rows_lo).then_inc(o_parts_ready, 1)
                nc.scalar.activation(s_part[:, :, :], o_ps[:, :, 0, :], ACT.Identity, scale=rows_hi).then_inc(o_parts_ready, 1)

            def q_round(st):
                for g in range(GROUPS):
                    act.wait_ge(stack_loaded[g], 16 * STACK_DMAS * st.a)
                act.wait_ge(q_done, st.a + 1)
                nc.scalar.activation(qk[:, :, Q_HI, :], dense[QQ % 2][:, :, :], ACT.Copy, scale=QSCALE).then_inc(qk_hi_ready, 1)

            def k_round(st):
                act.wait_ge(k_done, st.a + 1)
                nc.scalar.activation(qk[:, :, K_HI, :], dense[KK % 2][:, :, :], ACT.Copy).then_inc(qk_hi_ready, 1)

            def o_round(st):
                act.wait_ge(o_normed, 2 * (st.n + 1))
                act.wait_ge(wo_done, st.n)
                nc.scalar.activation(on_hi[:, :, :], o_norm[:, :, :], ACT.Copy).then_inc(on_hi_ready, 1)

            def square_x1(st):
                act.wait_ge(x1_ready, st.n + 1)
                act.wait_ge(norm_hi[1], st.n)
                act.wait_ge(norm_lo[1], st.n)
                nc.scalar.activation(norm_sq[1][:, :, :], x1[:, :, :], ACT.Square).then_inc(squares[1], 1)

            def place_v(st):
                act.wait_ge(v_done, st.s + 1)
                if st.looped or st.s >= 2:
                    act.wait_ge(pv_done, CHUNKS * (st.s - 1))
                for e in range(2):
                    src = dense[VV % 2][:, :, P * e:P * e + P].rearrange("p t (s d) -> p t s d", d=DH)
                    dst = v_aug[1 - st.parity][:, :, e, :, DH * e:DH * e + DH]
                    nc.scalar.activation(dst, src, ACT.Copy).then_inc(v_ready, 1)

            def emit(st):
                A, S, C, N, F = (b is not None for b in (st.a, st.s, st.c, st.n, st.f))
                if st.first:
                    split_hi(ATTN)
                    act.wait_ge(const_loaded, 16)
                    act.wait_ge(filled, FILLS)
                if st.at(1):
                    for w in range(4):
                        act.wait_ge(w_lo_done[w], 1)
                if N:
                    o_parts(st)
                if F:
                    tanh(st, 0)
                if C:
                    exps(st, 0)
                if F:
                    tanh(st, 1)
                    act_round(st, 0)
                if C:
                    exps(st, 1)
                if F:
                    tanh(st, 2)
                    act_round(st, 1)
                    tanh(st, 3)
                    act_round(st, 2)
                if C:
                    exps(st, 2)
                if F:
                    act_round(st, 3)
                if S:
                    place_v(st)
                if A:
                    norm_round(st, 0, st.a)
                if N:
                    o_round(st)
                if F:
                    tanh(st, 4)
                if C:
                    exps(st, 3)
                if F:
                    act_round(st, 4)
                if N:
                    square_x1(st)
                if A:
                    q_round(st)
                if C:
                    exps(st, 4)
                if A:
                    k_round(st)
                if F:
                    tanh(st, 5)
                if C:
                    exps(st, 5)
                if F:
                    tanh(st, 6)
                    act_round(st, 5)
                    tanh(st, 7)
                    act_round(st, 6)
                if C:
                    exps(st, 6)
                if F:
                    act_round(st, 7)
                if C:
                    exps(st, 7)
                if N:
                    norm_round(st, 1, st.n)
                if st.at(-1):
                    split_hi(GATE)
                if st.at(0):
                    split_hi(HID)
                    split_hi(OUT)

            steps(act, emit)

        @block.vector
        def _(dve):
            def split_lo(w):
                dve.wait_ge(w_hi_done[w], 1)
                nc.vector.tensor_tensor(w_lo_sb[w][:, :, :], raw_view(w), w_hi_sb[w][:, :, :].bitcast(F32),
                                        ALU.subtract).then_inc(w_lo_done[w], 1)

            def stats_turn(st, n, b):
                bank = (STAT1 if n == 0 else STAT2) % 2
                dve.wait_ge(stats_done[n], b + 1)
                dve.wait_ge(newton_step[n], NEWTON_STEPS * b)
                nc.vector.transpose(norm_tr[n][:, :, :].rearrange("p a c -> p (a c)"), dense[bank][:, 0, :]) \
                    .then_inc(stats_turned[n], 1)
                dve.wait_ge(stats_turned[n], b + 1)
                nc.vector.tensor_scalar(newton[n][:, 3, :], norm_tr[n][:, :, 0], EPS, None, ALU.add).then_inc(newton_step[n], 1)
                dve.wait_ge(newton_step[n], NEWTON_STEPS * b + 1)
                nc.vector.tensor_scalar(newton[n][:, 0, :], newton[n][:, 3, :], -0.5, None, ALU.mult).then_inc(newton_step[n], 1)
                nc.vector.tensor_scalar(newton[n][:, 1, :].bitcast(I32), newton[n][:, 3, :].bitcast(I32), -0.5, RSQRT_MAGIC,
                                        ALU.mult, ALU.add).then_inc(newton_step[n], 1)

            def normalise(st, n, b):
                dve.wait_ge(newton_step[n], NEWTON_STEPS * (b + 1))
                dve.wait_ge(x_scaled[n], b)
                nc.vector.transpose(norm_inv[:, :], newton[n][:, 1, :].unsqueeze(2).broadcast_to([P, T // 32, 32])) \
                    .then_inc(inv_spread[n], 1)
                dve.wait_ge(inv_spread[n], b + 1)
                dve.wait_ge(norm_hi[n], b)
                dve.wait_ge(norm_lo[n], b)
                src = x_sb[:, :, tokens(b)] if n == 0 else x1[:, :, :]
                nc.vector.tensor_tensor(norm_x[n][:, :, :], src, norm_inv[:, :].unsqueeze(1).broadcast_to([P, KT, T]),
                                        ALU.mult).then_inc(x_scaled[n], 1)
                dve.wait_ge(x_scaled[n], b + 1)
                for k in range(KT):
                    scale = gb[:, (2 * n) * KT + k, bass.ds(b, 1)]
                    shift = gb[:, (2 * n + 1) * KT + k, bass.ds(b, 1)]
                    nc.vector.tensor_scalar(norm_y[n][:, k, :], norm_x[n][:, k, :], scale, shift, ALU.mult, ALU.add) \
                        .then_inc(norm_ready[n], 1)

            def maxima(st, chunk):
                g, half = chunk // 2, chunk % 2
                dve.wait_ge(scores_done, CHUNKS * st.s + chunk + 1)
                nc.vector.tensor_reduce(m_raw[:, half, :, 2 * g:2 * g + 2], s_ps[:, :, :, :], AX.X, ALU.max).then_inc(maxed, 1)

            def gated(st, m):
                bank = UP_UNITS[m] % 2
                dve.wait_ge(tanh_ready, HT * st.f + m + 1)
                nc.vector.scalar_tensor_tensor(th[:, m % 2, :], th[:, m % 2, :], 1.0, dense[bank][:, 0, :], ALU.add, ALU.mult) \
                    .then_inc(silu_ready, 1)
                dve.wait_ge(silu_ready, HT * st.f + m + 1)
                dve.wait_ge(act_hi_ready, F_START + HT * st.f + max(m - 3, 0))
                dve.wait_ge(act_lo_ready, F_START + HT * st.f + max(m - 3, 0))
                nc.vector.tensor_tensor(act_f[:, m % 4, :], th[:, m % 2, :], dense[bank][:, 1, :], ALU.mult) \
                    .then_inc(act_ready, 1)

            def invert(st, pair):
                dve.wait_ge(s_spread, st.n + 1)
                nc.vector.reciprocal(s_recip[:, pair, :], s_bcast[:, pair, :]).then_inc(s_inverted, 1)

            def pack(st):
                dve.wait_ge(o_parts_ready, 2 * (st.n + 1))
                dve.wait_ge(on_hi_ready, st.n)
                dve.wait_ge(on_lo_ready, st.n)
                nc.vector.scalar_tensor_tensor(o_pack[:, :, :], o_ps[:, :, 1, :], rows_hi, o_part[:, :, :],
                                               ALU.mult, ALU.add).then_inc(o_packed, 1)
                nc.vector.scalar_tensor_tensor(s_pack[:, :, :], o_ps[:, :, 1, :], rows_lo, s_part[:, :, :],
                                               ALU.mult, ALU.add).then_inc(o_packed, 1)

            def swap_sums(st):
                dve.wait_ge(const_loaded, 16)
                dve.wait_ge(o_packed, 2 * (st.n + 1))
                nc.vector.stream_shuffle(s_bcast[:, :, :], s_pack[:, :, :], [(p + DH) % 32 for p in range(32)]) \
                    .then_inc(s_spread, 1)

            def divide(st):
                for pair in range(2):
                    dve.wait_ge(s_inverted, 2 * st.n + pair + 1)
                    nc.vector.tensor_tensor(o_norm[:, pair, :], o_pack[:, pair, :], s_recip[:, pair, :], ALU.mult) \
                        .then_inc(o_normed, 1)

            def q_rest(st):
                dve.wait_ge(qk_hi_ready, 2 * st.a + 1)
                nc.vector.scalar_tensor_tensor(qk[:, :, Q_LO, :], dense[QQ % 2][:, :, :], QSCALE,
                                               qk[:, :, Q_HI, :].bitcast(F32), ALU.mult, ALU.subtract).then_inc(qk_lo_ready, 1)

            def k_rest(st):
                dve.wait_ge(qk_hi_ready, 2 * st.a + 2)
                nc.vector.tensor_tensor(qk[:, :, K_LO, :], dense[KK % 2][:, :, :], qk[:, :, K_HI, :].bitcast(F32),
                                        ALU.subtract).then_inc(qk_lo_ready, 1)

            def add_x(st):
                dve.wait_ge(wo_done, st.n + 1)
                dve.wait_ge(squares[1], st.n)
                dve.wait_ge(resid_ready, st.n)
                nc.vector.tensor_tensor(x1[:, :, :], dense[WO % 2][:, :, :], x_sb[:, :, tokens(st.n)], ALU.add).then_inc(x1_ready, 1)

            def split_maxima(st):
                dve.wait_ge(maxed, CHUNKS * (st.s + 1))
                dve.wait_ge(m_turned, st.s)
                nc.vector.tensor_copy(m_split[:, :, :, 0, :], m_raw[:, :, :, :]).then_inc(m_hi_ready, 1)
                dve.wait_ge(m_hi_ready, st.s + 1)
                nc.vector.tensor_tensor(m_split[:, :, :, 1, :], m_raw[:, :, :, :], m_split[:, :, :, 0, :].bitcast(F32),
                                        ALU.subtract).then_inc(m_split_ready, 1)

            def take_max_rows(st):
                dve.wait_ge(m_turned, st.s + 1)
                dve.wait_ge(m_loaded, 16 * st.s)
                nc.vector.tensor_copy(m_rows[:, :], dense[MT % 2][0:32, 0, :]).then_inc(m_rows_ready, 1)

            def result(st):
                dve.wait_ge(f2_done, st.f + 1)
                dve.wait_ge(resid_ready, st.f + 1)
                dve.wait_ge(y_stored, STORE_START + 16 * st.f)
                nc.vector.scalar_tensor_tensor(y_sb, dense[F2 % 2][:, :, :], 0.5, resid[:, st.parity, :, :],
                                               ALU.mult, ALU.add).then_inc(y_ready, 1)

            nc.vector.memset(mean_w[:, :], 1.0 / D).then_inc(filled, 1)
            nc.vector.memset(zero_rows[:, :], 0.0).then_inc(filled, 1)
            dve.wait_ge(gb_product, 1)
            dve.wait_ge(cond_loaded, 16 * 3)
            nc.vector.tensor_tensor(gb[:, :, :], s_ps[:, 0, 0, 0:4 * KT * B].rearrange("p (a b) -> p a b", b=B),
                                    cb_sb[:, :].unsqueeze(2).broadcast_to([P, 4 * KT, B]), ALU.add).then_inc(gb_ready, 1)
            dve.wait_ge(gb_ready, 1)
            for n in range(3):
                dve.wait_ge(x_loaded[n], 16)
            dve.wait_ge(const_loaded, 16)

            def emit(st):
                A, S, C, N, F = (b is not None for b in (st.a, st.s, st.c, st.n, st.f))
                if S:
                    maxima(st, 0)
                if N:
                    pack(st)
                if F:
                    gated(st, 0)
                if N:
                    swap_sums(st)
                if A:
                    stats_turn(st, 0, st.a)
                if N:
                    invert(st, 0)
                if F:
                    gated(st, 1)
                if S:
                    maxima(st, 1)
                if F:
                    gated(st, 2)
                if N:
                    invert(st, 1)
                if F:
                    gated(st, 3)
                if S:
                    maxima(st, 2)
                if N:
                    divide(st)
                if A:
                    normalise(st, 0, st.a)
                if S:
                    maxima(st, 3)
                if F:
                    gated(st, 4)
                if N:
                    add_x(st)
                if S:
                    maxima(st, 4)
                if st.first:
                    split_lo(ATTN)
                if A:
                    q_rest(st)
                    k_rest(st)
                if S:
                    maxima(st, 5)
                if N:
                    stats_turn(st, 1, st.n)
                if F:
                    gated(st, 5)
                    gated(st, 6)
                if S:
                    maxima(st, 6)
                if F:
                    gated(st, 7)
                if S:
                    maxima(st, 7)
                    split_maxima(st)
                if N:
                    normalise(st, 1, st.n)
                if S:
                    take_max_rows(st)
                if F:
                    result(st)
                if st.at(-1):
                    split_lo(GATE)
                if st.at(0):
                    split_lo(HID)
                    split_lo(OUT)

            steps(dve, emit)

        @block.gpsimd
        def _(pool):
            for n in range(2):
                nc.gpsimd.memset(v_aug[n][:, :, :, :, :], 1.0).then_inc(filled, 1)
            nc.gpsimd.memset(three_halves[:, :], 1.5).then_inc(filled, 1)
            pool.wait_ge(filled, FILLS)
            for n in range(3):
                pool.wait_ge(x_loaded[n], 16)

            def square_x(a):
                pool.wait_ge(norm_hi[0], a)
                pool.wait_ge(norm_lo[0], a)
                nc.gpsimd.tensor_tensor(norm_sq[0][:, :, :], x_sb[:, :, tokens(a)], x_sb[:, :, tokens(a)], ALU.mult) \
                    .then_inc(squares[0], 1)
                add_squares(0, a)

            def add_squares(n, b):
                pool.wait_ge(squares[n], b + 1)
                pool.wait_ge(stats_done[n], b)
                nc.gpsimd.tensor_tensor(norm_sum[n][:, :], norm_sq[n][:, 0, :], norm_sq[n][:, 1, :], ALU.add) \
                    .then_inc(square_sums[n], 1)

            def newtons(n, b):
                v_half, y, w = (newton[n][:, k, :] for k in range(3))
                step = 3
                for _ in range(NEWTONS):
                    for op in (lambda: nc.gpsimd.tensor_tensor(w, y, y, ALU.mult),
                               lambda: nc.gpsimd.tensor_tensor(w, w, v_half, ALU.mult),
                               lambda: nc.gpsimd.tensor_tensor(w, w, three_halves[:, :], ALU.add),
                               lambda: nc.gpsimd.tensor_tensor(y, y, w, ALU.mult)):
                        pool.wait_ge(newton_step[n], NEWTON_STEPS * b + step)
                        op().then_inc(newton_step[n], 1)
                        step += 1

            def norm_rest(st, n, b):
                hi, lo = (h_hi[:, st.parity], h_lo[:, st.parity]) if n == 0 else (g_hi, g_lo)
                pool.wait_ge(norm_hi[n], b + 1)
                norm_buffer_free(pool, st, n)
                nc.gpsimd.tensor_tensor(lo[:, :, :], norm_y[n][:, :, :], hi[:, :, :].bitcast(F32), ALU.subtract) \
                    .then_inc(norm_lo[n], 1)

            def act_rest(st, m):
                pool.wait_ge(act_hi_ready, F_START + HT * st.f + m + 1)
                nc.gpsimd.tensor_tensor(act_lo[:, m, :], act_f[:, m % 4, :], act_hi[:, m, :].bitcast(F32), ALU.subtract) \
                    .then_inc(act_lo_ready, 1)

            def o_rest(st):
                pool.wait_ge(on_hi_ready, st.n + 1)
                pool.wait_ge(wo_done, st.n)
                nc.gpsimd.tensor_tensor(on_lo[:, :, :], o_norm[:, :, :], on_hi[:, :, :].bitcast(F32), ALU.subtract) \
                    .then_inc(on_lo_ready, 1)

            def residual(st):
                pool.wait_ge(x1_ready, st.n + 1)
                if st.looped or st.n >= 2:
                    pool.wait_ge(y_ready, F_START + st.n - 1)
                nc.gpsimd.tensor_tensor(resid[:, 1 - st.parity, :, :], x1[:, :, :], x_sb[:, :, tokens(st.n)], ALU.add) \
                    .then_inc(resid_ready, 1)

            def emit(st):
                A, S, C, N, F = (b is not None for b in (st.a, st.s, st.c, st.n, st.f))
                if st.at(1):
                    for w in range(4):
                        pool.wait_ge(w_lo_done[w], 1)
                if A:
                    square_x(st.a)
                    newtons(0, st.a)
                if F:
                    act_rest(st, 0)
                    act_rest(st, 1)
                    act_rest(st, 2)
                if A:
                    norm_rest(st, 0, st.a)
                if N:
                    o_rest(st)
                if F:
                    act_rest(st, 3)
                if N:
                    add_squares(1, st.n)
                if F:
                    act_rest(st, 4)
                if N:
                    residual(st)
                    newtons(1, st.n)
                if F:
                    act_rest(st, 5)
                    act_rest(st, 6)
                    act_rest(st, 7)
                if N:
                    norm_rest(st, 1, st.n)

            steps(pool, emit)


def kernel(x, cond_256, L0_cond_Wq, L0_cond_Wk, L0_cond_Wv, L0_cond_Wo, L0_cond_g1w, L0_cond_g1b, L0_cond_b1w, L0_cond_b1b,
           L0_cond_g2w, L0_cond_g2b, L0_cond_b2w, L0_cond_b2b, L0_cond_gate_w, L0_cond_hid_w, L0_cond_out_w):
    import numpy as np
    import concourse.bacc as bacc
    from concourse.bass_utils import run_bass_kernel_spmd

    def contraction_major(w_t, tiles):
        return np.ascontiguousarray(w_t.reshape(tiles, P, -1).transpose(1, 0, 2))

    w = {k: np.asarray(v) for k, v in dict(q=L0_cond_Wq, k=L0_cond_Wk, v=L0_cond_Wv, o=L0_cond_Wo).items()}
    wv = w["v"].T.reshape(D, 2, 2, 4, DH).transpose(0, 2, 1, 3, 4).reshape(D, D)
    wo = w["o"].T.reshape(2, 2, 4, DH, D).transpose(0, 2, 1, 3, 4).reshape(D, D)
    attn = contraction_major(np.concatenate([w["q"].T, w["k"].T, wv, wo], axis=1), KT)
    conds = [np.asarray(v) for v in (L0_cond_g1w, L0_cond_b1w, L0_cond_g2w, L0_cond_b2w)]
    biases = [np.asarray(v).reshape(KT, P) for v in (L0_cond_g1b, L0_cond_b1b, L0_cond_g2b, L0_cond_b2b)]
    rows = np.arange(P) % 32 < DH
    consts = np.concatenate([np.eye(P, dtype=np.float32), rows[:, None].astype(np.float32), (~rows)[:, None].astype(np.float32)], axis=1)
    score_rows = np.zeros((32, SLOTS, T), np.float32)
    for n in range(32):
        score_rows[n, n % SLOTS, :] = -1.0
    arrays = {
        "x_t": np.ascontiguousarray(np.asarray(x).reshape(B * T, KT, P).transpose(2, 1, 0)),
        "cond_t": np.ascontiguousarray(np.asarray(cond_256).T),
        "cond_w": np.ascontiguousarray(np.stack([c.T for c in conds], axis=1)),
        "cond_b": np.ascontiguousarray(np.concatenate(biases, axis=0).T),
        "w_attn": attn.reshape(P, -1),
        "w_gate": contraction_major(np.asarray(L0_cond_gate_w).T, KT).reshape(P, -1),
        "w_hid": contraction_major(np.asarray(L0_cond_hid_w).T, KT).reshape(P, -1),
        "w_out": contraction_major(np.asarray(L0_cond_out_w).T, HT).reshape(P, -1),
        "consts": consts,
        "score_rows": score_rows,
    }
    nc = bacc.Bacc("TRN2", target_bir_lowering=False, num_devices=1)
    args = [nc.dram_tensor(name, a.shape, mybir.dt.from_np(a.dtype), kind="ExternalInput").ap() for name, a in arrays.items()]
    out = nc.dram_tensor("out_t", (P, KT, B * T), F32, kind="ExternalOutput").ap()
    layer_kernel(nc, *args, out)
    r = run_bass_kernel_spmd(nc, [arrays], core_ids=[0])
    y = r.results[0]["out_t"]
    return y.transpose(2, 1, 0).reshape(B, T, D)
```

```python
from contextlib import ExitStack

import concourse.bass as bass
from concourse import mybir

F32 = mybir.dt.float32
F32R = mybir.dt.float32r
I32 = mybir.dt.int32
ALU = mybir.AluOpType
ACT = mybir.ActivationFunctionType
AX = mybir.AxisListType

P = 128
B, T, D = 8, 256, 256
HEADS, DH = 16, 16
HIDDEN = 1024
DT = 64
KT = D // P
TT = T // P
HT = HIDDEN // P
SLOTS = HEADS // 2
GROUPS = 4
CHUNKS = 8
EPS = 1e-6
QSCALE = 1.0 / 4.0
LOOP_FROM, LOOP_TO = 2, 6
STACK_DMAS = 6
RSQRT_MAGIC = float(0x5F3759DF)

VV, F4, F5, F6, WO, F7, STAT2, QQ, KK, F2A, F2B, F0, F1, F2, F3, MT = range(16)
UP_UNITS = (F0, F1, F2, F3, F4, F5, F6, F7)
DOWN_UNITS = (F2A, F2B)
FILLS = 5
NEWTONS = 3
NEWTON_STEPS = 3 + 4 * NEWTONS
BLOCKS = T // 32
ROOT_GROUPS = ((0, 1), (1, 3), (4, 4))


class Step:

    def __init__(self, i, parity, looped):
        self.i, self.parity, self.looped = i, parity, looped
        inside = (lambda b: True) if looped else (lambda b: 0 <= b < B)
        self.a = i + 2 if inside(i + 2) else None
        self.s = i + 1 if inside(i + 1) else None
        self.c = i if inside(i) else None
        self.n = i - 1 if inside(i - 1) else None
        self.f = i - 2 if inside(i - 2) else None
        self.first = not looped and i == -2

    def at(self, i):
        return not self.looped and self.i == i


def steps(engine, emit):
    for i in range(-2, LOOP_FROM):
        emit(Step(i, i % 2, False))
    with engine.Fori(LOOP_FROM // 2, LOOP_TO // 2) as pair:
        for u in range(2):
            emit(Step(pair * 2 + u, u, True))
    for i in range(LOOP_TO, B + 2):
        emit(Step(i, i % 2, False))


Y_START = 1
STORE_START = 16


def root_steps(group):
    return sum(count + 2 + 4 * NEWTONS for _, count in ROOT_GROUPS[:group + 1])


def variances_through(b):
    group = max(g for g, (first, _) in enumerate(ROOT_GROUPS) if first <= b)
    return root_steps(group - 1) + b - ROOT_GROUPS[group][0] + 1


def group_of(st):
    return len(ROOT_GROUPS) - 1 if st.looped else max(g for g, (first, _) in enumerate(ROOT_GROUPS) if first <= st.a)


def layer_kernel(nc, x_t, cond_t, cond_w, cond_b, w_attn, w_gate, w_hid, w_out, consts, score_rows, out_t):
    ctx = ExitStack()
    with ctx:
        def sb(name, shape, dt=F32):
            return ctx.enter_context(nc.sbuf_tensor(name, shape, dt))

        def pb(name, shape):
            return ctx.enter_context(nc.psum_tensor(name, shape, F32))

        def sem(name):
            return ctx.enter_context(nc.semaphore(name))

        x_sb = sb("x_sb", [P, KT, B * T])
        ct_sb = sb("ct_sb", [DT, B])
        cb_sb = sb("cb_sb", [P, 4 * KT])
        const_sb = sb("const_sb", [P, P + 2])
        ident, rows_lo, rows_hi = const_sb[:, 0:P], const_sb[:, P:P + 1], const_sb[:, P + 1:P + 2]
        mean_w = sb("mean_w", [P, P])
        three_halves = sb("three_halves", [P, B * BLOCKS])
        roots = sb("roots", [P, 4, B * BLOCKS])
        x_root = sb("x_root", [P, BLOCKS])
        zero_rows = sb("zero_rows", [32, T])
        gb = sb("gb", [P, 4 * KT, B])
        raw = [sb(f"raw{n}", [P, 2048]) for n in range(3)]
        attn_hi, attn_lo = sb("attn_hi", [P, KT, 4 * D], F32R), sb("attn_lo", [P, KT, 4 * D], F32R)
        gate_hi, gate_lo = sb("gate_hi", [P, KT, HIDDEN], F32R), sb("gate_lo", [P, KT, HIDDEN], F32R)
        hid_hi, hid_lo = sb("hid_hi", [P, KT, HIDDEN], F32R), sb("hid_lo", [P, KT, HIDDEN], F32R)
        out_hi, out_lo = sb("out_hi", [P, HT, D], F32R), sb("out_lo", [P, HT, D], F32R)

        norm_sum = sb("norm_sum", [P, T])
        norm_tr = sb("norm_tr", [P, BLOCKS, 32])
        newton = sb("newton", [P, 4, BLOCKS])
        norm_inv = sb("norm_inv", [P, T])
        norm_x = [sb(f"norm_x{n}", [P, KT, T]) for n in range(2)]
        norm_sq = norm_y = norm_x
        h_hi, h_lo = sb("h_hi", [P, 2, KT, T], F32R), sb("h_lo", [P, 2, KT, T], F32R)
        g_hi, g_lo = sb("g_hi", [P, KT, T], F32R), sb("g_lo", [P, KT, T], F32R)
        qk = sb("qk", [P, KT, 4, T], F32R)
        Q_HI, Q_LO, K_HI, K_LO = range(4)
        stack = [sb(f"stack{n}", [P, SLOTS, 2, T], F32R) for n in range(2)]
        v_aug = [sb(f"v_aug{n}", [P, TT, 2, SLOTS, 32]) for n in range(2)]
        m_raw = sb("m_raw", [P, TT, 2, SLOTS])
        m_split = sb("m_split", [P, TT, 2, 2, SLOTS], F32R)
        m_rows = sb("m_rows", [32, T])
        probs = sb("probs", [P, 2, 2, 2, T])
        on_hi, on_lo = sb("on_hi", [P, 2, T], F32R), sb("on_lo", [P, 2, T], F32R)
        s_pack = sb("s_pack", [P, 2, T])
        o_norm = s_pack
        turned_x = s_pack[:, :, :].rearrange("p e (a c) -> p e a c", c=32)
        act_hi, act_lo = sb("act_hi", [P, HT, T], F32R), sb("act_lo", [P, HT, T], F32R)
        cw_sb = probs[0:DT, 0, :, :, :].rearrange("p a b n -> p (a b) n")
        probs_flat = probs[:, :, :, :, :].rearrange("p a b c n -> p (a b c n)")

        def place(n, k, tiles):
            return raw[n][:, k * T:(k + tiles) * T].rearrange("p (a t) -> p a t", t=T)

        act_f, s_bcast, x1 = place(0, 0, 4), place(0, 4, 2), place(0, 6, 2)
        resid = raw[1][:, 0:4 * T].rearrange("p (b a t) -> p b a t", b=2, t=T)
        y_sb, o_pack = place(1, 4, 2), place(1, 6, 2)
        th, o_part, s_part = place(2, 0, 2), place(2, 2, 2), place(2, 4, 2)
        s_recip = s_part
        x_squares = [norm_x[1][:, :, :],
                     probs_flat[:, 0:2 * 3 * T].rearrange("p (k n) -> p k n", k=KT),
                     probs_flat[:, 0:2 * 4 * T].rearrange("p (k n) -> p k n", k=KT)]

        s_ps = pb("s_ps", [P, 2, 2, T])
        st_ps = pb("st_ps", [P, 2, 2, T])
        o_ps = pb("o_ps", [P, 2, 2, T])
        dense = [pb(f"dense{n}", [P, 2, T]) for n in range(2)]
        st_flat, o_flat = (t[:, :, :, :].rearrange("p a b n -> p (a b) n") for t in (st_ps, o_ps))
        x_means = [st_flat[:, 0], o_flat[:, 0], o_flat[:, 1], o_flat[:, 2]] + [st_flat[:, n] for n in range(4)]

        x_loaded = [sem(f"x_loaded{n}") for n in range(3)]
        cond_loaded, const_loaded, score_rows_loaded = sem("cond_loaded"), sem("const_loaded"), sem("score_rows_loaded")
        score_rows_staged = sem("score_rows_staged")
        w_loaded = [sem(f"w_loaded{n}") for n in range(5)]
        w_hi_done = [sem(f"w_hi_done{n}") for n in range(5)]
        w_lo_done = [sem(f"w_lo_done{n}") for n in range(5)]
        filled, gb_product, gb_ready = sem("filled"), sem("gb_product"), sem("gb_ready")
        x_squared, x_averaged, x_turned, root_step, root_taken = (
            sem("x_squared"), sem("x_averaged"), sem("x_turned"), sem("root_step"), sem("root_taken"))
        squares, square_sums, stats_done, stats_turned, newton_step = (
            sem("squares"), sem("square_sums"), sem("stats_done"), sem("stats_turned"), sem("newton_step"))
        inv_spread = [sem(f"inv_spread{n}") for n in range(2)]
        x_scaled = [sem(f"x_scaled{n}") for n in range(2)]
        norm_ready = [sem(f"norm_ready{n}") for n in range(2)]
        norm_hi = [sem(f"norm_hi{n}") for n in range(2)]
        norm_lo = [sem(f"norm_lo{n}") for n in range(2)]
        q_done, k_done, v_done = sem("q_done"), sem("k_done"), sem("v_done")
        qk_hi_ready, qk_lo_ready, v_ready = sem("qk_hi_ready"), sem("qk_lo_ready"), sem("v_ready")
        stack_loaded = [sem(f"stack_loaded{n}") for n in range(GROUPS)]
        scores_done, maxed, m_hi_ready, m_split_ready = sem("scores_done"), sem("maxed"), sem("m_hi_ready"), sem("m_split_ready")
        m_turned, m_rows_ready, m_loaded = sem("m_turned"), sem("m_rows_ready"), sem("m_loaded")
        scores_t_done, exp_done, pv_done = sem("scores_t_done"), sem("exp_done"), sem("pv_done")
        o_parts_ready, o_packed, s_spread, s_inverted, o_normed = (
            sem("o_parts_ready"), sem("o_packed"), sem("s_spread"), sem("s_inverted"), sem("o_normed"))
        on_hi_ready, on_lo_ready = sem("on_hi_ready"), sem("on_lo_ready")
        wo_done, x1_ready, resid_ready = sem("wo_done"), sem("x1_ready"), sem("resid_ready")
        f1_done, tanh_ready, silu_ready, act_ready = sem("f1_done"), sem("tanh_ready"), sem("silu_ready"), sem("act_ready")
        act_hi_ready, act_lo_ready, f2_done, y_ready, y_stored = (
            sem("act_hi_ready"), sem("act_lo_ready"), sem("f2_done"), sem("y_ready"), sem("y_stored"))

        QK_W, VO_W, GATE, HID, OUT = range(5)
        attn_raw = raw[0][:, :].rearrange("p (a n) -> p a n", a=KT)
        w_raw = [attn_raw[:, :, 0:2 * D], attn_raw[:, :, 2 * D:4 * D],
                 raw[1][:, :].rearrange("p (a n) -> p a n", a=KT), raw[2][:, :].rearrange("p (a n) -> p a n", a=KT),
                 raw[0][:, :].rearrange("p (a n) -> p a n", a=HT)]
        w_hi_sb = [attn_hi[:, :, 0:2 * D], attn_hi[:, :, 2 * D:4 * D], gate_hi[:, :, :], hid_hi[:, :, :], out_hi[:, :, :]]
        w_lo_sb = [attn_lo[:, :, 0:2 * D], attn_lo[:, :, 2 * D:4 * D], gate_lo[:, :, :], hid_lo[:, :, :], out_lo[:, :, :]]

        def stacked(st, b, g):
            zeros = b + 1 - 2 if st.looped else max(b + 1 - 2, 0)
            return 16 * (STACK_DMAS * (b + 1) + zeros)

        def tokens(b):
            return bass.ds(b * T, T)

        def norm_buffer_free(engine, st, n):
            if n == 0 and (st.looped or st.a >= 2):
                engine.wait_ge(v_done, st.a - 1)
            if n == 1:
                engine.wait_ge(f1_done, HT * st.n)

        block = ctx.enter_context(nc.Block())

        @block.sync
        def _(sp):
            def load_x(n, lo, hi):
                sp.dma_start(x_sb[:, :, lo * T:hi * T], x_t[:, :, lo * T:hi * T]).then_inc(x_loaded[n], 16)

            load_x(0, 0, 1)
            sp.sem_inc(y_ready, Y_START)
            sp.sem_inc(y_stored, STORE_START)
            sp.dma_start(const_sb[:, :], consts).then_inc(const_loaded, 16)
            for w, part in ((QK_W, slice(0, 2 * D)), (VO_W, slice(2 * D, 4 * D))):
                sp.dma_start(w_raw[w], w_attn[:, :, part]).then_inc(w_loaded[w], 16)
                if w == QK_W:
                    load_x(1, 1, 4)
            sp.dma_start(raw[1][:, :], w_gate).then_inc(w_loaded[GATE], 16)
            staged = raw[2][0:32, :].rearrange("p (s t) -> p s t", t=T)
            sp.dma_start(staged, score_rows).then_inc(score_rows_staged, 16)
            load_x(2, 4, B)
            sp.wait_ge(score_rows_staged, 16)
            sp.wait_ge(filled, FILLS)
            for n in range(2):
                sp.dma_start(stack[n][3:P:4, :, 1, :].bitcast(F32), staged).then_inc(score_rows_loaded, 16)
                sp.dma_start(stack[n][3:P:4, :, 0, :].bitcast(F32), zero_rows[:, :].unsqueeze(1).broadcast_to([32, SLOTS, T])) \
                    .then_inc(score_rows_loaded, 16)
            sp.wait_ge(score_rows_loaded, 64)
            sp.dma_start(raw[2][:, :], w_hid).then_inc(w_loaded[HID], 16)

            def stack_group(st, g):
                if st.c is not None:
                    sp.wait_ge(scores_t_done, CHUNKS * st.c + 2 * g + 2)
                if g == 0:
                    sp.wait_ge(qk_lo_ready, 2 * (st.a + 1))
                dst = stack[st.parity]
                if st.c is not None:
                    sp.dma_start(dst[3:P:4, 2 * g:2 * g + 2, 0, :].bitcast(F32),
                                 zero_rows[:, :].unsqueeze(1).broadcast_to([32, 2, T])).then_inc(stack_loaded[g], 16)
                for sl in range(2):
                    slot = 2 * g + sl
                    j = slot % 4
                    src = qk[32 * j:32 * j + 32, slot // 4, :, :].bitcast(F32)
                    for r, pair in enumerate((src[:, Q_HI:K_HI + 1:2, :], src[:, Q_LO:K_HI + 1, :], src[:, Q_HI:K_LO + 1:3, :])):
                        sp.dma_start(dst[r:P:4, slot, :, :].bitcast(F32), pair).then_inc(stack_loaded[g], 16)

            def send_max_rows(st):
                sp.wait_ge(m_rows_ready, st.s + 1)
                sp.dma_start(stack[1 - st.parity][3:P:4, :, 0, :].bitcast(F32),
                             m_rows[:, :].unsqueeze(1).broadcast_to([32, SLOTS, T])).then_inc(m_loaded, 16)

            def store(st):
                sp.wait_ge(y_ready, Y_START + KT * (st.f + 1))
                sp.dma_start(out_t[:, :, tokens(st.f)], y_sb).then_inc(y_stored, 16)

            def emit(st):
                A, S, F = (b is not None for b in (st.a, st.s, st.f))
                if A:
                    stack_group(st, 0)
                if F:
                    store(st)
                if A:
                    stack_group(st, 1)
                if S:
                    send_max_rows(st)
                if A:
                    stack_group(st, 2)
                    stack_group(st, 3)
                if st.first:
                    sp.wait_ge(w_lo_done[QK_W], 1)
                    sp.wait_ge(w_lo_done[VO_W], 1)
                    sp.dma_start(raw[0][:, :], w_out).then_inc(w_loaded[OUT], 16)

            steps(sp, emit)
            sp.wait_ge(y_stored, STORE_START + 16 * B)

        @block.tensor
        def _(pe):
            read_signal = {QQ: (2, qk_lo_ready, 2, 1), KK: (2, qk_lo_ready, 2, 2), VV: (1, v_ready, 2, 2),
                           MT: (1, m_rows_ready, 1, 1), WO: (-1, x1_ready, 1, 1), STAT2: (-1, stats_turned, 1, 1)}
            read_signal |= {unit: (-1 if m < HT // 2 else -2, act_ready, HT, m + 1) for m, unit in enumerate(UP_UNITS)}
            read_signal |= {unit: (-2, y_ready, KT, Y_START + m + 1) for m, unit in enumerate(DOWN_UNITS)}

            def dense_bank(st, unit):
                i, before = st.i, unit - 2
                while True:
                    if before < 0:
                        i, before = i - 1, before + len(read_signal)
                    ahead, signal, per_batch, within = read_signal[before]
                    batch = i + ahead
                    if st.looped or 0 <= batch < B:
                        pe.wait_ge(signal, per_batch * batch + within)
                        break
                    if i < -2:
                        break
                    before -= 2
                return dense[unit % 2]

            def product(out, passes):
                for n, (w, m) in enumerate(passes):
                    last = nc.tensor.matmul(out, w, m, start=(n == 0), stop=(n == len(passes) - 1))
                return last

            def three(w_hi, w_lo, m_hi, m_lo, ks):
                return [pair for k in ks for pair in ((w_hi(k), m_hi(k)), (w_hi(k), m_lo(k)), (w_lo(k), m_hi(k)))]

            def columns(w, first):
                return lambda k: w[:, k, first:first + P]

            def x_variances(group):
                first, count = ROOT_GROUPS[group]
                pe.wait_ge(x_squared, group + 1)
                pe.wait_ge(x_turned, first)
                for n in range(count):
                    product(x_means[first + n], [(mean_w[:, :], x_squares[group][:, k, n * T:(n + 1) * T]) for k in range(KT)]) \
                        .then_inc(x_averaged, 1)

            def stats(st):
                d = dense_bank(st, STAT2)
                pe.wait_ge(square_sums, st.n + 1)
                product(d[:, 0, :], [(mean_w[:, :], norm_sum[:, :])]).then_inc(stats_done, 1)

            def project(st, unit, first_col, done):
                d = dense_bank(st, unit)
                h = st.parity
                for m in range(KT):
                    last = product(d[:, m, :], three(columns(attn_hi, first_col + m * P), columns(attn_lo, first_col + m * P),
                                                     lambda k: h_hi[:, h, k, :], lambda k: h_lo[:, h, k, :], range(KT)))
                last.then_inc(done, 1)

            def values(st):
                d = dense_bank(st, VV)
                h = 1 - st.parity
                for t in range(TT):
                    tok = slice(t * P, t * P + P)
                    last = product(d[:, t, :], three(lambda k: h_hi[:, h, k, tok], lambda k: h_lo[:, h, k, tok],
                                                     lambda k: attn_hi[:, k, 2 * D:3 * D], lambda k: attn_lo[:, k, 2 * D:3 * D],
                                                     range(KT)))
                last.then_inc(v_done, 1)

            def scores(st, chunk):
                g, half = chunk // 2, chunk % 2
                if half == 0:
                    pe.wait_ge(stack_loaded[g], stacked(st, st.s, g))
                pe.wait_ge(maxed, CHUNKS * st.s + chunk)
                buf = stack[1 - st.parity]
                for sl in range(2):
                    for par in range(2):
                        win = slice(64 * par, 64 * par + 64)
                        last = product(s_ps[:, par, sl, :], [(buf[win, 2 * g + sl, 0, half * P:half * P + P],
                                                              buf[win, 2 * g + sl, 1, :])])
                last.then_inc(scores_done, 1)

            def scores_t(st, chunk):
                g, half = chunk // 2, chunk % 2
                if chunk == 0:
                    pe.wait_ge(m_loaded, 16 * (st.c + 1))
                pe.wait_ge(exp_done, CHUNKS * st.c + chunk)
                buf = stack[st.parity]
                for sl in range(2):
                    for par in range(2):
                        win = slice(64 * par, 64 * par + 64)
                        last = product(st_ps[:, par, sl, :], [(buf[win, 2 * g + sl, 1, half * P:half * P + P],
                                                               buf[win, 2 * g + sl, 0, :])])
                last.then_inc(scores_t_done, 1)

            def probs_v(st, chunk):
                g, half = chunk // 2, chunk % 2
                if chunk == 0:
                    pe.wait_ge(v_ready, 2 * (st.c + 1))
                if chunk == 0 and (st.looped or st.c > 0):
                    pe.wait_ge(o_packed, 4 * st.c - 2)
                if chunk == CHUNKS // 2:
                    pe.wait_ge(o_packed, 4 * st.c)
                pe.wait_ge(exp_done, CHUNKS * st.c + chunk + 1)
                for j in range(4):
                    last = nc.tensor.matmul(o_ps[32 * j:32 * j + 32, g // 2, g % 2, :],
                                            v_aug[st.parity][:, half, g % 2, 4 * (g // 2) + j, :],
                                            probs[:, chunk % 2, j % 2, j // 2, :], start=(half == 0), stop=(half == 1))
                last.then_inc(pv_done, 1)

            def max_rows(st):
                d = dense_bank(st, MT)
                pe.wait_ge(m_split_ready, st.s + 1)
                for t in range(TT):
                    lhs = m_split[:, t, :, :, :].rearrange("p a b s -> p (a b s)").bitcast(F32)
                    last = product(d[0:32, 0, t * P:t * P + P], [(lhs, ident)])
                last.then_inc(m_turned, 1)

            def out_proj(st):
                d = dense_bank(st, WO)
                pe.wait_ge(on_hi_ready, 2 * (st.n + 1))
                pe.wait_ge(on_lo_ready, 2 * (st.n + 1))
                for m in range(KT):
                    last = product(d[:, m, :], three(columns(attn_hi, 3 * D + m * P), columns(attn_lo, 3 * D + m * P),
                                                     lambda k: on_hi[:, k, :], lambda k: on_lo[:, k, :], range(2)))
                last.then_inc(wo_done, 1)

            def ffn_up(st, m):
                d = dense_bank(st, UP_UNITS[m])
                if m == 0:
                    pe.wait_ge(norm_hi[1], st.n + 1)
                    pe.wait_ge(norm_lo[1], st.n + 1)
                for half, (hi, lo) in enumerate(((gate_hi, gate_lo), (hid_hi, hid_lo))):
                    last = product(d[:, half, :], three(columns(hi, m * P), columns(lo, m * P),
                                                        lambda k: g_hi[:, k, :], lambda k: g_lo[:, k, :], range(KT)))
                last.then_inc(f1_done, 1)

            def ffn_down(st, m):
                d = dense_bank(st, DOWN_UNITS[m])
                for half in range(2):
                    if m == 0:
                        pe.wait_ge(act_hi_ready, HT * st.f + 4 * (half + 1))
                        pe.wait_ge(act_lo_ready, HT * st.f + 4 * (half + 1))
                    passes = three(columns(out_hi, m * P), columns(out_lo, m * P),
                                   lambda k: act_hi[:, k, :], lambda k: act_lo[:, k, :], range(4 * half, 4 * half + 4))
                    for n, (w, mov) in enumerate(passes):
                        last = nc.tensor.matmul(d[:, m, :], w, mov, start=(half == 0 and n == 0),
                                                stop=(half == 1 and n == len(passes) - 1))
                last.then_inc(f2_done, 1)

            pe.wait_ge(cond_loaded, 16 * 3)
            for n in range(4 * KT):
                last = product(s_ps[:, 0, 0, n * B:n * B + B], [(cw_sb[:, n // KT, (n % KT) * P:(n % KT) * P + P], ct_sb[:, :])])
            last.then_inc(gb_product, 1)
            pe.wait_ge(filled, FILLS)
            pe.wait_ge(const_loaded, 16)
            x_variances(0)

            def wait_norm_x(st):
                if st.first:
                    pe.wait_ge(w_lo_done[QK_W], 1)
                pe.wait_ge(norm_hi[0], st.a + 1)
                pe.wait_ge(norm_lo[0], st.a + 1)

            def emit(st):
                A, S, C, N, F = (b is not None for b in (st.a, st.s, st.c, st.n, st.f))
                if st.at(-1):
                    pe.wait_ge(gb_ready, 1)
                    pe.wait_ge(w_lo_done[VO_W], 1)
                    values(st)
                    pe.wait_ge(score_rows_loaded, 64)
                if st.at(0):
                    pe.wait_ge(x_turned, B)
                if st.at(1):
                    for w in (GATE, HID, OUT):
                        pe.wait_ge(w_lo_done[w], 1)
                if S:
                    scores(st, 0)
                if S and not st.at(-1):
                    values(st)
                if F:
                    ffn_up(st, 4)
                    ffn_up(st, 5)
                if C:
                    scores_t(st, 0)
                if F:
                    ffn_up(st, 6)
                if S:
                    scores(st, 1)
                if C:
                    scores_t(st, 1)
                if st.at(-1):
                    x_variances(2)
                if C:
                    probs_v(st, 0)
                if N:
                    out_proj(st)
                if C:
                    scores_t(st, 2)
                if F:
                    ffn_up(st, 7)
                if A:
                    wait_norm_x(st)
                if S:
                    scores(st, 2)
                if C:
                    probs_v(st, 1)
                    scores_t(st, 3)
                    probs_v(st, 2)
                if S:
                    scores(st, 3)
                if N:
                    stats(st)
                if A:
                    project(st, QQ, 0, q_done)
                if C:
                    probs_v(st, 3)
                if S:
                    scores(st, 4)
                if A:
                    project(st, KK, D, k_done)
                if C:
                    scores_t(st, 4)
                if F:
                    ffn_down(st, 0)
                if S:
                    scores(st, 5)
                if C:
                    scores_t(st, 5)
                if st.first:
                    x_variances(1)
                if F:
                    ffn_down(st, 1)
                if C:
                    probs_v(st, 4)
                    probs_v(st, 5)
                    scores_t(st, 6)
                if S:
                    scores(st, 6)
                if N:
                    ffn_up(st, 0)
                    ffn_up(st, 1)
                if C:
                    scores_t(st, 7)
                if S:
                    scores(st, 7)
                if N:
                    ffn_up(st, 2)
                    ffn_up(st, 3)
                if C:
                    probs_v(st, 6)
                    probs_v(st, 7)
                if S:
                    max_rows(st)

            steps(pe, emit)

        @block.scalar
        def _(act):
            act.dma_start(ct_sb[:, :], cond_t).then_inc(cond_loaded, 16)
            act.dma_start(cw_sb[:, :, :], cond_w).then_inc(cond_loaded, 16)
            act.dma_start(cb_sb[:, :], cond_b).then_inc(cond_loaded, 16)

            def split_hi(w):
                act.wait_ge(w_loaded[w], 16)
                nc.scalar.activation(w_hi_sb[w], w_raw[w], ACT.Copy).then_inc(w_hi_done[w], 1)

            def norm_round(st, n, b):
                dst = h_hi[:, st.parity, :, :] if n == 0 else g_hi[:, :, :]
                act.wait_ge(norm_ready[n], 2 * (b + 1))
                norm_buffer_free(act, st, n)
                nc.scalar.activation(dst, norm_y[n][:, :, :], ACT.Copy).then_inc(norm_hi[n], 1)

            def exps(st, chunk):
                act.wait_ge(scores_t_done, CHUNKS * st.c + chunk + 1)
                if chunk >= 2 or st.looped or st.c > 0:
                    act.wait_ge(pv_done, CHUNKS * st.c + chunk - 1)
                nc.scalar.activation(probs[:, chunk % 2, :, :, :], st_ps[:, :, :, :], ACT.Exp).then_inc(exp_done, 1)

            def square_x(group):
                first, count = ROOT_GROUPS[group]
                act.wait_ge(x_loaded[group], 16)
                if group == 1:
                    act.wait_ge(gb_product, 1)
                if group == 2:
                    act.wait_ge(x_averaged, first)
                nc.scalar.activation(x_squares[group], x_sb[:, :, first * T:(first + count) * T], ACT.Square).then_inc(x_squared, 1)

            def tanh(st, m):
                b = st.n if m < HT // 2 else st.f
                act.wait_ge(f1_done, HT * b + m + 1)
                if m >= 2 or st.looped or b > 0:
                    act.wait_ge(act_ready, HT * b + m - 1)
                nc.scalar.activation(th[:, m % 2, :], dense[UP_UNITS[m] % 2][:, 0, :], ACT.Tanh, scale=0.5).then_inc(tanh_ready, 1)

            def act_round(st, m):
                act.wait_ge(act_ready, HT * (st.n if m < HT // 2 - 1 else st.f) + m + 1)
                nc.scalar.activation(act_hi[:, m, :], act_f[:, m % 4, :], ACT.Copy).then_inc(act_hi_ready, 1)

            def o_parts(b, pair):
                act.wait_ge(pv_done, CHUNKS * b + 4 * (pair + 1))
                if not isinstance(b, int) or b > 0:
                    act.wait_ge(o_normed, 2 * b + pair - 1)
                nc.scalar.activation(o_part[:, pair, :], o_ps[:, pair, 0, :], ACT.Identity, scale=rows_lo).then_inc(o_parts_ready, 1)
                nc.scalar.activation(s_part[:, pair, :], o_ps[:, pair, 0, :], ACT.Identity, scale=rows_hi).then_inc(o_parts_ready, 1)

            def q_round(st):
                if not st.first:
                    for g in range(GROUPS):
                        act.wait_ge(stack_loaded[g], stacked(st, st.a - 1, g))
                act.wait_ge(q_done, st.a + 1)
                nc.scalar.activation(qk[:, :, Q_HI, :], dense[QQ % 2][:, :, :], ACT.Copy, scale=QSCALE).then_inc(qk_hi_ready, 1)

            def k_round(st):
                act.wait_ge(k_done, st.a + 1)
                nc.scalar.activation(qk[:, :, K_HI, :], dense[KK % 2][:, :, :], ACT.Copy).then_inc(qk_hi_ready, 1)

            def o_round(b, pair):
                act.wait_ge(o_normed, 2 * b + pair + 1)
                act.wait_ge(wo_done, b)
                nc.scalar.activation(on_hi[:, pair, :], o_norm[:, pair, :], ACT.Copy).then_inc(on_hi_ready, 1)

            def square_x1(st):
                act.wait_ge(x1_ready, st.n + 1)
                act.wait_ge(norm_hi[1], st.n)
                act.wait_ge(norm_lo[1], st.n)
                nc.scalar.activation(norm_sq[1][:, :, :], x1[:, :, :], ACT.Square).then_inc(squares, 1)

            def place_v(st):
                act.wait_ge(v_done, st.s + 1)
                if st.looped or st.s >= 2:
                    act.wait_ge(pv_done, CHUNKS * (st.s - 1))
                for e in range(2):
                    src = dense[VV % 2][:, :, P * e:P * e + P].rearrange("p t (s d) -> p t s d", d=DH)
                    dst = v_aug[1 - st.parity][:, :, e, :, DH * e:DH * e + DH]
                    nc.scalar.activation(dst, src, ACT.Copy).then_inc(v_ready, 1)

            square_x(0)
            split_hi(QK_W)
            act.wait_ge(const_loaded, 16)
            act.wait_ge(filled, FILLS)

            def emit(st):
                A, S, C, N, F = (b is not None for b in (st.a, st.s, st.c, st.n, st.f))
                if st.at(-1):
                    place_v(st)
                if st.at(0):
                    for w in range(5):
                        act.wait_ge(w_lo_done[w], 1)
                if S and not st.at(-1):
                    place_v(st)
                if st.at(-1):
                    split_hi(HID)
                if F:
                    tanh(st, 4)
                    act_round(st, 3)
                    tanh(st, 5)
                if C:
                    exps(st, 0)
                if F:
                    act_round(st, 4)
                if N:
                    o_round(st.n, 1)
                if F:
                    tanh(st, 6)
                    act_round(st, 5)
                if C:
                    exps(st, 1)
                if A:
                    norm_round(st, 0, st.a)
                if C:
                    exps(st, 2)
                if N:
                    square_x1(st)
                if st.first:
                    split_hi(VO_W)
                if F:
                    tanh(st, 7)
                    act_round(st, 6)
                if C:
                    exps(st, 3)
                if F:
                    act_round(st, 7)
                if st.first:
                    square_x(1)
                if A:
                    q_round(st)
                if C:
                    o_parts(st.c, 0)
                if A:
                    k_round(st)
                if C:
                    exps(st, 4)
                    exps(st, 5)
                if N:
                    norm_round(st, 1, st.n)
                if C:
                    exps(st, 6)
                if N:
                    tanh(st, 0)
                    tanh(st, 1)
                    act_round(st, 0)
                if C:
                    exps(st, 7)
                    o_round(st.c, 0)
                if N:
                    tanh(st, 2)
                if st.at(-1):
                    split_hi(OUT)
                if st.first:
                    split_hi(GATE)
                    square_x(2)
                if N:
                    tanh(st, 3)
                if C:
                    o_parts(st.c, 1)
                if N:
                    act_round(st, 1)
                    act_round(st, 2)

            steps(act, emit)

        @block.vector
        def _(dve):
            def split_lo(w):
                dve.wait_ge(w_hi_done[w], 1)
                nc.vector.tensor_tensor(w_lo_sb[w], w_raw[w], w_hi_sb[w].bitcast(F32),
                                        ALU.subtract).then_inc(w_lo_done[w], 1)

            def first_guess(y, v_half, v, count):
                nc.vector.tensor_scalar(v_half, v, -0.5, None, ALU.mult).then_inc(count, 1)
                nc.vector.tensor_scalar(y.bitcast(I32), v.bitcast(I32), -0.5, RSQRT_MAGIC, ALU.mult, ALU.add).then_inc(count, 1)

            def x_roots(group):
                first, count = ROOT_GROUPS[group]
                done = root_steps(group - 1)
                dve.wait_ge(x_averaged, first + count)
                for b in range(first, first + count):
                    part = slice(b * BLOCKS, (b + 1) * BLOCKS)
                    if b >= 2:
                        dve.wait_ge(root_step, variances_through(b - 2))
                    nc.vector.transpose(turned_x[:, b % 2].rearrange("p a c -> p (a c)"), x_means[b]).then_inc(x_turned, 1)
                    dve.wait_ge(x_turned, b + 1)
                    nc.vector.tensor_scalar(roots[:, 3, part], turned_x[:, b % 2, :, 0], EPS, None, ALU.add).then_inc(root_step, 1)
                dve.wait_ge(root_step, done + count)
                part = slice(first * BLOCKS, (first + count) * BLOCKS)
                first_guess(roots[:, 1, part], roots[:, 0, part], roots[:, 3, part], root_step)

            def stats_turn(st):
                b = st.n
                dve.wait_ge(stats_done, b + 1)
                dve.wait_ge(newton_step, NEWTON_STEPS * b)
                nc.vector.transpose(norm_tr[:, :, :].rearrange("p a c -> p (a c)"), dense[STAT2 % 2][:, 0, :]) \
                    .then_inc(stats_turned, 1)
                dve.wait_ge(stats_turned, b + 1)
                nc.vector.tensor_scalar(newton[:, 3, :], norm_tr[:, :, 0], EPS, None, ALU.add).then_inc(newton_step, 1)
                dve.wait_ge(newton_step, NEWTON_STEPS * b + 1)
                first_guess(newton[:, 1, :], newton[:, 0, :], newton[:, 3, :], newton_step)

            def spread_roots(st, n, b):
                if n == 0:
                    dve.wait_ge(root_step, root_steps(group_of(st)))
                    dve.wait_ge(inv_spread[0], b)
                    nc.vector.tensor_copy(x_root[:, :], roots[:, 1, bass.ds(b * BLOCKS, BLOCKS)]).then_inc(root_taken, 1)
                    dve.wait_ge(root_taken, b + 1)
                    root = x_root[:, :]
                else:
                    dve.wait_ge(newton_step, NEWTON_STEPS * (b + 1))
                    root = newton[:, 1, :]
                dve.wait_ge(x_scaled[n], b)
                if n == 0 and (st.looped or b >= 4):
                    dve.wait_ge(x_scaled[1], b - 3)
                if n == 1:
                    dve.wait_ge(x_scaled[0], b + 4 if st.looped or b + 4 <= B else B)
                nc.vector.transpose(norm_inv[:, :], root.unsqueeze(2).broadcast_to([P, BLOCKS, 32])).then_inc(inv_spread[n], 1)

            def normalise(st, n, b):
                spread_roots(st, n, b)
                dve.wait_ge(inv_spread[n], b + 1)
                dve.wait_ge(norm_hi[n], b)
                dve.wait_ge(norm_lo[n], b)
                src = x_sb[:, :, tokens(b)] if n == 0 else x1[:, :, :]
                nc.vector.tensor_tensor(norm_x[n][:, :, :], src, norm_inv[:, :].unsqueeze(1).broadcast_to([P, KT, T]),
                                        ALU.mult).then_inc(x_scaled[n], 1)
                dve.wait_ge(x_scaled[n], b + 1)
                for k in range(KT):
                    scale = gb[:, (2 * n) * KT + k, bass.ds(b, 1)]
                    shift = gb[:, (2 * n + 1) * KT + k, bass.ds(b, 1)]
                    nc.vector.tensor_scalar(norm_y[n][:, k, :], norm_x[n][:, k, :], scale, shift, ALU.mult, ALU.add) \
                        .then_inc(norm_ready[n], 1)

            def maxima(st, chunk):
                g, half = chunk // 2, chunk % 2
                dve.wait_ge(scores_done, CHUNKS * st.s + chunk + 1)
                nc.vector.tensor_reduce(m_raw[:, half, :, 2 * g:2 * g + 2], s_ps[:, :, :, :], AX.X, ALU.max).then_inc(maxed, 1)

            def gated(st, m):
                bank = UP_UNITS[m] % 2
                b = st.n if m < HT // 2 else st.f
                dve.wait_ge(tanh_ready, HT * b + m + 1)
                nc.vector.scalar_tensor_tensor(th[:, m % 2, :], th[:, m % 2, :], 1.0, dense[bank][:, 0, :], ALU.add, ALU.mult) \
                    .then_inc(silu_ready, 1)
                dve.wait_ge(silu_ready, HT * b + m + 1)
                if m >= 4 or st.looped or b > 0:
                    dve.wait_ge(act_hi_ready, HT * b + m - 3)
                    dve.wait_ge(act_lo_ready, HT * b + m - 3)
                nc.vector.tensor_tensor(act_f[:, m % 4, :], th[:, m % 2, :], dense[bank][:, 1, :], ALU.mult) \
                    .then_inc(act_ready, 1)

            def pack(b, pair):
                dve.wait_ge(o_parts_ready, 4 * b + 2 * pair + 2)
                if not isinstance(b, int) or b > 0:
                    dve.wait_ge(on_hi_ready, 2 * b + pair - 1)
                    dve.wait_ge(on_lo_ready, 2 * b + pair - 1)
                nc.vector.scalar_tensor_tensor(o_pack[:, pair, :], o_ps[:, pair, 1, :], rows_hi, o_part[:, pair, :],
                                               ALU.mult, ALU.add).then_inc(o_packed, 1)
                nc.vector.scalar_tensor_tensor(s_pack[:, pair, :], o_ps[:, pair, 1, :], rows_lo, s_part[:, pair, :],
                                               ALU.mult, ALU.add).then_inc(o_packed, 1)

            def swap_sums(b, pair):
                dve.wait_ge(const_loaded, 16)
                dve.wait_ge(o_packed, 4 * b + 2 * pair + 2)
                nc.vector.stream_shuffle(s_bcast[:, pair, :], s_pack[:, pair, :], [(p + DH) % 32 for p in range(32)]) \
                    .then_inc(s_spread, 1)

            def invert(b, pair):
                dve.wait_ge(s_spread, 2 * b + pair + 1)
                nc.vector.reciprocal(s_recip[:, pair, :], s_bcast[:, pair, :]).then_inc(s_inverted, 1)

            def divide(b, pair):
                dve.wait_ge(s_inverted, 2 * b + pair + 1)
                nc.vector.tensor_tensor(o_norm[:, pair, :], o_pack[:, pair, :], s_recip[:, pair, :], ALU.mult) \
                    .then_inc(o_normed, 1)

            def q_rest(st):
                dve.wait_ge(qk_hi_ready, 2 * st.a + 1)
                nc.vector.scalar_tensor_tensor(qk[:, :, Q_LO, :], dense[QQ % 2][:, :, :], QSCALE,
                                               qk[:, :, Q_HI, :].bitcast(F32), ALU.mult, ALU.subtract).then_inc(qk_lo_ready, 1)

            def k_rest(st):
                dve.wait_ge(qk_hi_ready, 2 * st.a + 2)
                nc.vector.tensor_tensor(qk[:, :, K_LO, :], dense[KK % 2][:, :, :], qk[:, :, K_HI, :].bitcast(F32),
                                        ALU.subtract).then_inc(qk_lo_ready, 1)

            def add_x(st):
                dve.wait_ge(wo_done, st.n + 1)
                dve.wait_ge(squares, st.n)
                dve.wait_ge(resid_ready, st.n)
                nc.vector.tensor_tensor(x1[:, :, :], dense[WO % 2][:, :, :], x_sb[:, :, tokens(st.n)], ALU.add).then_inc(x1_ready, 1)

            def split_maxima(st):
                dve.wait_ge(maxed, CHUNKS * (st.s + 1))
                dve.wait_ge(m_turned, st.s)
                nc.vector.tensor_copy(m_split[:, :, :, 0, :], m_raw[:, :, :, :]).then_inc(m_hi_ready, 1)
                dve.wait_ge(m_hi_ready, st.s + 1)
                nc.vector.tensor_tensor(m_split[:, :, :, 1, :], m_raw[:, :, :, :], m_split[:, :, :, 0, :].bitcast(F32),
                                        ALU.subtract).then_inc(m_split_ready, 1)

            def take_max_rows(st):
                dve.wait_ge(m_turned, st.s + 1)
                dve.wait_ge(m_loaded, 16 * st.s)
                nc.vector.tensor_copy(m_rows[:, :], dense[MT % 2][0:32, 0, :]).then_inc(m_rows_ready, 1)

            def result(st, m):
                dve.wait_ge(f2_done, 2 * st.f + m + 1)
                dve.wait_ge(resid_ready, st.f + 1)
                dve.wait_ge(y_stored, STORE_START + 16 * st.f)
                nc.vector.scalar_tensor_tensor(y_sb[:, m, :], dense[DOWN_UNITS[m] % 2][:, m, :], 0.5, resid[:, st.parity, m, :],
                                               ALU.mult, ALU.add).then_inc(y_ready, 1)

            nc.vector.memset(mean_w[:, :], 1.0 / D).then_inc(filled, 1)
            nc.vector.memset(zero_rows[:, :], 0.0).then_inc(filled, 1)
            x_roots(0)
            dve.wait_ge(gb_product, 1)
            dve.wait_ge(cond_loaded, 16 * 3)
            nc.vector.tensor_tensor(gb[:, :, :], s_ps[:, 0, 0, 0:4 * KT * B].rearrange("p (a b) -> p a b", b=B),
                                    cb_sb[:, :].unsqueeze(2).broadcast_to([P, 4 * KT, B]), ALU.add).then_inc(gb_ready, 1)
            split_lo(QK_W)
            dve.wait_ge(gb_ready, 1)
            dve.wait_ge(x_loaded[0], 16)
            dve.wait_ge(const_loaded, 16)

            def emit(st):
                A, S, C, N, F = (b is not None for b in (st.a, st.s, st.c, st.n, st.f))
                if st.at(-1):
                    dve.wait_ge(x_loaded[1], 16)
                if st.at(1):
                    dve.wait_ge(x_loaded[2], 16)
                if F:
                    gated(st, 4)
                if S:
                    maxima(st, 0)
                if N:
                    divide(st.n, 1)
                if F:
                    gated(st, 5)
                    gated(st, 6)
                if A:
                    normalise(st, 0, st.a)
                if S:
                    maxima(st, 1)
                if N:
                    add_x(st)
                if S:
                    maxima(st, 2)
                if F:
                    gated(st, 7)
                if S:
                    maxima(st, 3)
                if N:
                    stats_turn(st)
                if st.at(-1):
                    x_roots(2)
                if A:
                    q_rest(st)
                if S:
                    maxima(st, 4)
                if C:
                    pack(st.c, 0)
                if A:
                    k_rest(st)
                if st.first:
                    split_lo(VO_W)
                if N:
                    normalise(st, 1, st.n)
                if st.first:
                    x_roots(1)
                if C:
                    swap_sums(st.c, 0)
                if S:
                    maxima(st, 5)
                if F:
                    result(st, 0)
                if st.at(-1):
                    split_lo(HID)
                if F:
                    result(st, 1)
                if C:
                    invert(st.c, 0)
                if S:
                    maxima(st, 6)
                if N:
                    gated(st, 0)
                if C:
                    divide(st.c, 0)
                if N:
                    gated(st, 1)
                if S:
                    maxima(st, 7)
                if st.first:
                    split_lo(GATE)
                if N:
                    gated(st, 2)
                if S:
                    split_maxima(st)
                if N:
                    gated(st, 3)
                if S:
                    take_max_rows(st)
                if st.at(-1):
                    split_lo(OUT)
                if C:
                    pack(st.c, 1)
                    swap_sums(st.c, 1)
                    invert(st.c, 1)

            steps(dve, emit)

        @block.gpsimd
        def _(pool):
            for n in range(2):
                nc.gpsimd.memset(v_aug[n][:, :, :, :, :], 1.0).then_inc(filled, 1)
            nc.gpsimd.memset(three_halves[:, :], 1.5).then_inc(filled, 1)
            pool.wait_ge(filled, FILLS)

            def newtons(y, v_half, w, count, done):
                for _ in range(NEWTONS):
                    for op in (lambda: nc.gpsimd.tensor_tensor(w, y, y, ALU.mult),
                               lambda: nc.gpsimd.tensor_tensor(w, w, v_half, ALU.mult),
                               lambda: nc.gpsimd.tensor_tensor(w, w, three_halves[:, 0:w.shape[-1]], ALU.add),
                               lambda: nc.gpsimd.tensor_tensor(y, y, w, ALU.mult)):
                        pool.wait_ge(count, done)
                        op().then_inc(count, 1)
                        done += 1

            def x_newtons(group):
                first, count = ROOT_GROUPS[group]
                part = slice(first * BLOCKS, (first + count) * BLOCKS)
                newtons(roots[:, 1, part], roots[:, 0, part], roots[:, 2, part], root_step, root_steps(group) - 4 * NEWTONS)

            def add_squares(st):
                pool.wait_ge(squares, st.n + 1)
                pool.wait_ge(stats_done, st.n)
                nc.gpsimd.tensor_tensor(norm_sum[:, :], norm_sq[1][:, 0, :], norm_sq[1][:, 1, :], ALU.add) \
                    .then_inc(square_sums, 1)

            def norm_rest(st, n, b):
                hi, lo = (h_hi[:, st.parity], h_lo[:, st.parity]) if n == 0 else (g_hi, g_lo)
                pool.wait_ge(norm_hi[n], b + 1)
                norm_buffer_free(pool, st, n)
                nc.gpsimd.tensor_tensor(lo[:, :, :], norm_y[n][:, :, :], hi[:, :, :].bitcast(F32), ALU.subtract) \
                    .then_inc(norm_lo[n], 1)

            def act_rest(st, m):
                pool.wait_ge(act_hi_ready, HT * (st.n if m < HT // 2 - 1 else st.f) + m + 1)
                nc.gpsimd.tensor_tensor(act_lo[:, m, :], act_f[:, m % 4, :], act_hi[:, m, :].bitcast(F32), ALU.subtract) \
                    .then_inc(act_lo_ready, 1)

            def o_rest(b, pair):
                pool.wait_ge(on_hi_ready, 2 * b + pair + 1)
                pool.wait_ge(wo_done, b)
                nc.gpsimd.tensor_tensor(on_lo[:, pair, :], o_norm[:, pair, :], on_hi[:, pair, :].bitcast(F32), ALU.subtract) \
                    .then_inc(on_lo_ready, 1)

            def residual(st):
                pool.wait_ge(x1_ready, st.n + 1)
                if st.looped or st.n >= 2:
                    pool.wait_ge(y_ready, Y_START + 2 * (st.n - 1))
                nc.gpsimd.tensor_tensor(resid[:, 1 - st.parity, :, :], x1[:, :, :], x_sb[:, :, tokens(st.n)], ALU.add) \
                    .then_inc(resid_ready, 1)

            x_newtons(0)

            def emit(st):
                A, S, C, N, F = (b is not None for b in (st.a, st.s, st.c, st.n, st.f))
                if st.at(1):
                    for n in range(3):
                        pool.wait_ge(x_loaded[n], 16)
                if F:
                    act_rest(st, 3)
                if N:
                    o_rest(st.n, 1)
                if F:
                    act_rest(st, 4)
                if A:
                    norm_rest(st, 0, st.a)
                if F:
                    act_rest(st, 5)
                if N:
                    add_squares(st)
                if F:
                    act_rest(st, 6)
                if st.at(-1):
                    x_newtons(2)
                if F:
                    act_rest(st, 7)
                if N:
                    newtons(newton[:, 1, :], newton[:, 0, :], newton[:, 2, :], newton_step, NEWTON_STEPS * st.n + 3)
                    residual(st)
                    norm_rest(st, 1, st.n)
                if C:
                    o_rest(st.c, 0)
                if N:
                    act_rest(st, 0)
                if st.first:
                    x_newtons(1)
                if N:
                    act_rest(st, 1)
                    act_rest(st, 2)

            steps(pool, emit)


def kernel(x, cond_256, L0_cond_Wq, L0_cond_Wk, L0_cond_Wv, L0_cond_Wo, L0_cond_g1w, L0_cond_g1b, L0_cond_b1w, L0_cond_b1b,
           L0_cond_g2w, L0_cond_g2b, L0_cond_b2w, L0_cond_b2b, L0_cond_gate_w, L0_cond_hid_w, L0_cond_out_w):
    import numpy as np
    import concourse.bacc as bacc
    from concourse.bass_utils import run_bass_kernel_spmd

    def contraction_major(w_t, tiles):
        return np.ascontiguousarray(w_t.reshape(tiles, P, -1).transpose(1, 0, 2))

    w = {k: np.asarray(v) for k, v in dict(q=L0_cond_Wq, k=L0_cond_Wk, v=L0_cond_Wv, o=L0_cond_Wo).items()}
    wv = w["v"].T.reshape(D, 2, 2, 4, DH).transpose(0, 2, 1, 3, 4).reshape(D, D)
    wo = w["o"].T.reshape(2, 2, 4, DH, D).transpose(0, 2, 1, 3, 4).reshape(D, D)
    attn = contraction_major(np.concatenate([w["q"].T, w["k"].T, wv, wo], axis=1), KT)
    conds = [np.asarray(v) for v in (L0_cond_g1w, L0_cond_b1w, L0_cond_g2w, L0_cond_b2w)]
    biases = [np.asarray(v).reshape(KT, P) for v in (L0_cond_g1b, L0_cond_b1b, L0_cond_g2b, L0_cond_b2b)]
    rows = np.arange(P) % 32 < DH
    consts = np.concatenate([np.eye(P, dtype=np.float32), rows[:, None].astype(np.float32), (~rows)[:, None].astype(np.float32)], axis=1)
    score_rows = np.zeros((32, SLOTS, T), np.float32)
    for n in range(32):
        score_rows[n, n % SLOTS, :] = -1.0
    arrays = {
        "x_t": np.ascontiguousarray(np.asarray(x).reshape(B * T, KT, P).transpose(2, 1, 0)),
        "cond_t": np.ascontiguousarray(np.asarray(cond_256).T),
        "cond_w": np.ascontiguousarray(np.stack([c.T for c in conds], axis=1)),
        "cond_b": np.ascontiguousarray(np.concatenate(biases, axis=0).T),
        "w_attn": attn,
        "w_gate": contraction_major(np.asarray(L0_cond_gate_w).T, KT).reshape(P, -1),
        "w_hid": contraction_major(np.asarray(L0_cond_hid_w).T, KT).reshape(P, -1),
        "w_out": contraction_major(np.asarray(L0_cond_out_w).T, HT).reshape(P, -1),
        "consts": consts,
        "score_rows": score_rows,
    }
    nc = bacc.Bacc("TRN2", target_bir_lowering=False, num_devices=1)
    args = [nc.dram_tensor(name, a.shape, mybir.dt.from_np(a.dtype), kind="ExternalInput").ap() for name, a in arrays.items()]
    out = nc.dram_tensor("out_t", (P, KT, B * T), F32, kind="ExternalOutput").ap()
    layer_kernel(nc, *args, out)
    r = run_bass_kernel_spmd(nc, [arrays], core_ids=[0])
    y = r.results[0]["out_t"]
    return y.transpose(2, 1, 0).reshape(B, T, D)
```

```python
from contextlib import ExitStack

import concourse.bass as bass
from concourse import mybir

F32 = mybir.dt.float32
F32R = mybir.dt.float32r
I32 = mybir.dt.int32
ALU = mybir.AluOpType
ACT = mybir.ActivationFunctionType
AX = mybir.AxisListType

P = 128
B, T, D = 8, 256, 256
HEADS, DH = 16, 16
HIDDEN = 1024
DT = 64
KT = D // P
TT = T // P
HT = HIDDEN // P
SLOTS = HEADS // 2
GROUPS = 4
CHUNKS = 8
EPS = 1e-6
QSCALE = 1.0 / 4.0
LOOP_FROM, LOOP_TO = 2, 6
STACK_DMAS = 6
RSQRT_MAGIC = float(0x5F3759DF)

VV, F4, F5, F6, WO, F7, STAT2, QQ, KK, F2A, F2B, F0, F1, F2, F3, MT = range(16)
UP_UNITS = (F0, F1, F2, F3, F4, F5, F6, F7)
DOWN_UNITS = (F2A, F2B)
DRAIN_BANK = {unit: m % 4 for m, unit in enumerate(UP_UNITS)} | {WO: 0, STAT2: 2, F2A: 0, F2B: 1}
FILLS = 5
NEWTONS = 3
NEWTON_STEPS = 3 + 4 * NEWTONS
BLOCKS = T // 32
ROOT_GROUPS = ((0, 1), (1, 3), (4, 4))


class Step:

    def __init__(self, i, parity, looped):
        self.i, self.parity, self.looped = i, parity, looped
        inside = (lambda b: True) if looped else (lambda b: 0 <= b < B)
        self.a = i + 2 if inside(i + 2) else None
        self.s = i + 1 if inside(i + 1) else None
        self.c = i if inside(i) else None
        self.n = i - 1 if inside(i - 1) else None
        self.f = i - 2 if inside(i - 2) else None
        self.first = not looped and i == -2
        self.drains = not looped and i >= B - 1

    def at(self, i):
        return not self.looped and self.i == i


def steps(engine, fill, steady, drain):
    for i in range(-2, 1):
        fill(Step(i, i % 2, False))
    for i in range(1, LOOP_FROM):
        steady(Step(i, i % 2, False))
    with engine.Fori(LOOP_FROM // 2, LOOP_TO // 2) as pair:
        for u in range(2):
            steady(Step(pair * 2 + u, u, True))
    for i in range(LOOP_TO, B - 1):
        steady(Step(i, i % 2, False))
    for i in range(B - 1, B + 2):
        drain(Step(i, i % 2, False))


Y_START = 1
STORE_START = 16


def root_steps(group):
    return sum(count + 2 + 4 * NEWTONS for _, count in ROOT_GROUPS[:group + 1])


def variances_through(b):
    group = max(g for g, (first, _) in enumerate(ROOT_GROUPS) if first <= b)
    return root_steps(group - 1) + b - ROOT_GROUPS[group][0] + 1


def group_of(st):
    return len(ROOT_GROUPS) - 1 if st.looped else max(g for g, (first, _) in enumerate(ROOT_GROUPS) if first <= st.a)


def layer_kernel(nc, x_t, cond_t, cond_w, cond_b, w_attn, w_gate, w_hid, w_out, consts, score_rows, out_t):
    ctx = ExitStack()
    with ctx:
        def sb(name, shape, dt=F32):
            return ctx.enter_context(nc.sbuf_tensor(name, shape, dt))

        def pb(name, shape):
            return ctx.enter_context(nc.psum_tensor(name, shape, F32))

        def sem(name):
            return ctx.enter_context(nc.semaphore(name))

        x_sb = sb("x_sb", [P, KT, B * T])
        ct_sb = sb("ct_sb", [DT, B])
        cb_sb = sb("cb_sb", [P, 4 * KT])
        const_sb = sb("const_sb", [P, P + 2])
        ident, rows_lo, rows_hi = const_sb[:, 0:P], const_sb[:, P:P + 1], const_sb[:, P + 1:P + 2]
        mean_w = sb("mean_w", [P, P])
        three_halves = sb("three_halves", [P, B * BLOCKS])
        roots = sb("roots", [P, 4, B * BLOCKS])
        x_root = sb("x_root", [P, BLOCKS])
        zero_rows = sb("zero_rows", [32, T])
        gb = sb("gb", [P, 4 * KT, B])
        raw = [sb(f"raw{n}", [P, 2048]) for n in range(3)]
        attn_hi, attn_lo = sb("attn_hi", [P, KT, 4 * D], F32R), sb("attn_lo", [P, KT, 4 * D], F32R)
        gate_hi, gate_lo = sb("gate_hi", [P, KT, HIDDEN], F32R), sb("gate_lo", [P, KT, HIDDEN], F32R)
        hid_hi, hid_lo = sb("hid_hi", [P, KT, HIDDEN], F32R), sb("hid_lo", [P, KT, HIDDEN], F32R)
        out_hi, out_lo = sb("out_hi", [P, HT, D], F32R), sb("out_lo", [P, HT, D], F32R)

        norm_sum = sb("norm_sum", [P, T])
        norm_tr = sb("norm_tr", [P, BLOCKS, 32])
        newton = sb("newton", [P, 4, BLOCKS])
        norm_inv = sb("norm_inv", [P, T])
        norm_x = [sb(f"norm_x{n}", [P, KT, T]) for n in range(2)]
        norm_sq = norm_y = norm_x
        h_hi, h_lo = sb("h_hi", [P, 2, KT, T], F32R), sb("h_lo", [P, 2, KT, T], F32R)
        g_hi, g_lo = sb("g_hi", [P, KT, T], F32R), sb("g_lo", [P, KT, T], F32R)
        qk = sb("qk", [P, KT, 4, T], F32R)
        Q_HI, Q_LO, K_HI, K_LO = range(4)
        stack = [sb(f"stack{n}", [P, SLOTS, 2, T], F32R) for n in range(2)]
        v_aug = [sb(f"v_aug{n}", [P, TT, 2, SLOTS, 32]) for n in range(2)]
        m_raw = sb("m_raw", [P, TT, 2, SLOTS])
        m_split = sb("m_split", [P, TT, 2, 2, SLOTS], F32R)
        m_rows = sb("m_rows", [32, T])
        probs = sb("probs", [P, 2, 2, 2, T])
        on_hi, on_lo = sb("on_hi", [P, 2, T], F32R), sb("on_lo", [P, 2, T], F32R)
        s_pack = sb("s_pack", [P, 2, T])
        o_norm = s_pack
        turned_x = s_pack[:, :, :].rearrange("p e (a c) -> p e a c", c=32)
        act_hi, act_lo = sb("act_hi", [P, HT, T], F32R), sb("act_lo", [P, HT, T], F32R)
        cw_sb = probs[0:DT, 0, :, :, :].rearrange("p a b n -> p (a b) n")
        probs_flat = probs[:, :, :, :, :].rearrange("p a b c n -> p (a b c n)")

        def place(n, k, tiles):
            return raw[n][:, k * T:(k + tiles) * T].rearrange("p (a t) -> p a t", t=T)

        act_f, s_bcast, x1 = place(0, 0, 4), place(0, 4, 2), place(0, 6, 2)
        resid = raw[1][:, 0:4 * T].rearrange("p (b a t) -> p b a t", b=2, t=T)
        y_sb, o_pack = place(1, 4, 2), place(1, 6, 2)
        th, o_part, s_part = place(2, 0, 2), place(2, 2, 2), place(2, 4, 2)
        s_recip = s_part
        x_squares = [norm_x[1][:, :, :],
                     probs_flat[:, 0:2 * 3 * T].rearrange("p (k n) -> p k n", k=KT),
                     probs_flat[:, 0:2 * 4 * T].rearrange("p (k n) -> p k n", k=KT)]

        s_ps = pb("s_ps", [P, 2, 2, T])
        st_ps = pb("st_ps", [P, 2, 2, T])
        o_ps = pb("o_ps", [P, 2, 2, T])
        dense = [pb(f"dense{n}", [P, 2, T]) for n in range(2)]
        st_flat, o_flat = (t[:, :, :, :].rearrange("p a b n -> p (a b) n") for t in (st_ps, o_ps))
        x_means = [st_flat[:, 0]] + [o_flat[:, n] for n in (0, 1, 2)] + [o_flat[:, n] for n in range(4)]

        x_loaded = [sem(f"x_loaded{n}") for n in range(3)]
        cond_loaded, const_loaded, score_rows_loaded = sem("cond_loaded"), sem("const_loaded"), sem("score_rows_loaded")
        score_rows_staged = sem("score_rows_staged")
        w_loaded = [sem(f"w_loaded{n}") for n in range(5)]
        w_hi_done = [sem(f"w_hi_done{n}") for n in range(5)]
        w_lo_done = [sem(f"w_lo_done{n}") for n in range(5)]
        filled, gb_product, gb_ready = sem("filled"), sem("gb_product"), sem("gb_ready")
        x_squared, x_averaged, x_turned, root_step, root_taken = (
            sem("x_squared"), sem("x_averaged"), sem("x_turned"), sem("root_step"), sem("root_taken"))
        squares, square_sums, stats_done, stats_turned, newton_step = (
            sem("squares"), sem("square_sums"), sem("stats_done"), sem("stats_turned"), sem("newton_step"))
        inv_spread = [sem(f"inv_spread{n}") for n in range(2)]
        x_scaled = [sem(f"x_scaled{n}") for n in range(2)]
        norm_ready = [sem(f"norm_ready{n}") for n in range(2)]
        norm_hi = [sem(f"norm_hi{n}") for n in range(2)]
        norm_lo = [sem(f"norm_lo{n}") for n in range(2)]
        q_done, k_done, v_done = sem("q_done"), sem("k_done"), sem("v_done")
        qk_hi_ready, qk_lo_ready, v_ready = sem("qk_hi_ready"), sem("qk_lo_ready"), sem("v_ready")
        stack_loaded = [sem(f"stack_loaded{n}") for n in range(GROUPS)]
        scores_done, maxed, m_hi_ready, m_split_ready = sem("scores_done"), sem("maxed"), sem("m_hi_ready"), sem("m_split_ready")
        m_turned, m_rows_ready, m_loaded = sem("m_turned"), sem("m_rows_ready"), sem("m_loaded")
        scores_t_done, exp_done, pv_done = sem("scores_t_done"), sem("exp_done"), sem("pv_done")
        o_parts_ready, o_packed, s_spread, s_inverted, o_normed = (
            sem("o_parts_ready"), sem("o_packed"), sem("s_spread"), sem("s_inverted"), sem("o_normed"))
        on_hi_ready, on_lo_ready = sem("on_hi_ready"), sem("on_lo_ready")
        wo_done, x1_ready, resid_ready = sem("wo_done"), sem("x1_ready"), sem("resid_ready")
        f1_done, tanh_ready, silu_ready, act_ready = sem("f1_done"), sem("tanh_ready"), sem("silu_ready"), sem("act_ready")
        act_hi_ready, act_lo_ready, f2_done, y_ready, y_stored = (
            sem("act_hi_ready"), sem("act_lo_ready"), sem("f2_done"), sem("y_ready"), sem("y_stored"))

        QK_W, VO_W, GATE, HID, OUT = range(5)
        attn_raw = raw[0][:, :].rearrange("p (a n) -> p a n", a=KT)
        w_raw = [attn_raw[:, :, 0:2 * D], attn_raw[:, :, 2 * D:4 * D],
                 raw[1][:, :].rearrange("p (a n) -> p a n", a=KT), raw[2][:, :].rearrange("p (a n) -> p a n", a=KT),
                 raw[0][:, :].rearrange("p (a n) -> p a n", a=HT)]
        w_hi_sb = [attn_hi[:, :, 0:2 * D], attn_hi[:, :, 2 * D:4 * D], gate_hi[:, :, :], hid_hi[:, :, :], out_hi[:, :, :]]
        w_lo_sb = [attn_lo[:, :, 0:2 * D], attn_lo[:, :, 2 * D:4 * D], gate_lo[:, :, :], hid_lo[:, :, :], out_lo[:, :, :]]

        def stacked(st, b, g):
            zeros = b + 1 - 2 if st.looped else max(b + 1 - 2, 0)
            return 16 * (STACK_DMAS * (b + 1) + zeros)

        def tokens(b):
            return bass.ds(b * T, T)

        def bank_number(st, unit):
            return DRAIN_BANK[unit] if st.drains else unit % 2

        def unit_bank(st, unit):
            n = bank_number(st, unit)
            return dense[n] if n < 2 else s_ps[:, n - 2]

        def score_bank(st, chunk):
            return st_ps if st.at(-1) and chunk % 2 == 1 else s_ps

        def norm_buffer_free(engine, st, n):
            if n == 0 and (st.looped or st.a >= 2):
                engine.wait_ge(v_done, st.a - 1)
            if n == 1:
                engine.wait_ge(f1_done, HT * st.n)

        block = ctx.enter_context(nc.Block())

        @block.sync
        def _(sp):
            def load_x(n, lo, hi):
                sp.dma_start(x_sb[:, :, lo * T:hi * T], x_t[:, :, lo * T:hi * T]).then_inc(x_loaded[n], 16)

            load_x(0, 0, 1)
            sp.sem_inc(y_ready, Y_START)
            sp.sem_inc(y_stored, STORE_START)
            sp.dma_start(ct_sb[:, :], cond_t).then_inc(cond_loaded, 16)
            sp.dma_start(cw_sb[:, :, :], cond_w).then_inc(cond_loaded, 16)
            sp.dma_start(cb_sb[:, :], cond_b).then_inc(cond_loaded, 16)
            sp.dma_start(const_sb[:, :], consts).then_inc(const_loaded, 16)
            for w, part in ((QK_W, slice(0, 2 * D)), (VO_W, slice(2 * D, 4 * D))):
                sp.dma_start(w_raw[w], w_attn[:, :, part]).then_inc(w_loaded[w], 16)
                if w == QK_W:
                    load_x(1, 1, 4)
            sp.dma_start(raw[1][:, :], w_gate).then_inc(w_loaded[GATE], 16)
            staged = raw[2][0:32, :].rearrange("p (s t) -> p s t", t=T)
            sp.dma_start(staged, score_rows).then_inc(score_rows_staged, 16)
            load_x(2, 4, B)
            sp.wait_ge(score_rows_staged, 16)
            sp.wait_ge(filled, FILLS)
            for n in range(2):
                sp.dma_start(stack[n][3:P:4, :, 1, :].bitcast(F32), staged).then_inc(score_rows_loaded, 16)
                sp.dma_start(stack[n][3:P:4, :, 0, :].bitcast(F32), zero_rows[:, :].unsqueeze(1).broadcast_to([32, SLOTS, T])) \
                    .then_inc(score_rows_loaded, 16)
            sp.wait_ge(score_rows_loaded, 64)
            sp.dma_start(raw[2][:, :], w_hid).then_inc(w_loaded[HID], 16)

            def stack_group(st, g):
                if st.c is not None:
                    sp.wait_ge(scores_t_done, CHUNKS * st.c + 2 * g + 2)
                if g == 0:
                    sp.wait_ge(qk_hi_ready, 2 * (st.a + 1))
                dst = stack[st.parity]
                if st.c is not None:
                    sp.dma_start(dst[3:P:4, 2 * g:2 * g + 2, 0, :].bitcast(F32),
                                 zero_rows[:, :].unsqueeze(1).broadcast_to([32, 2, T])).then_inc(stack_loaded[g], 16)
                for sl in range(2):
                    slot = 2 * g + sl
                    j = slot % 4
                    src = qk[32 * j:32 * j + 32, slot // 4, :, :].bitcast(F32)
                    for r, pair in enumerate((src[:, Q_HI:K_HI + 1:2, :], src[:, Q_LO:K_HI + 1, :], src[:, Q_HI:K_LO + 1:3, :])):
                        if slot == 0 and r == 1:
                            sp.wait_ge(qk_lo_ready, 2 * (st.a + 1))
                        sp.dma_start(dst[r:P:4, slot, :, :].bitcast(F32), pair).then_inc(stack_loaded[g], 16)

            def send_max_rows(st):
                sp.wait_ge(m_rows_ready, st.s + 1)
                sp.dma_start(stack[1 - st.parity][3:P:4, :, 0, :].bitcast(F32),
                             m_rows[:, :].unsqueeze(1).broadcast_to([32, SLOTS, T])).then_inc(m_loaded, 16)

            def store(st):
                sp.wait_ge(y_ready, Y_START + KT * (st.f + 1))
                sp.dma_start(out_t[:, :, tokens(st.f)], y_sb).then_inc(y_stored, 16)

            def fill(st):
                stack_group(st, 0)
                stack_group(st, 1)
                if st.s is not None:
                    send_max_rows(st)
                stack_group(st, 2)
                stack_group(st, 3)
                if st.first:
                    sp.wait_ge(w_lo_done[QK_W], 1)
                    sp.wait_ge(w_lo_done[VO_W], 1)
                    sp.dma_start(raw[0][:, :], w_out).then_inc(w_loaded[OUT], 16)

            def steady(st):
                if st.a is not None:
                    stack_group(st, 0)
                if st.f is not None:
                    store(st)
                if st.a is not None:
                    stack_group(st, 1)
                send_max_rows(st)
                if st.a is not None:
                    stack_group(st, 2)
                    stack_group(st, 3)

            def drain(st):
                store(st)

            steps(sp, fill, steady, drain)
            sp.wait_ge(y_stored, STORE_START + 16 * B)

        @block.tensor
        def _(pe):
            read_signal = {QQ: (2, qk_lo_ready, 2, 1), KK: (2, qk_lo_ready, 2, 2), VV: (1, v_ready, 2, 2),
                           MT: (1, m_rows_ready, 1, 1), WO: (-1, x1_ready, 1, 1), STAT2: (-1, stats_turned, 1, 1)}
            read_signal |= {unit: (-1 if m < HT // 2 else -2, act_ready, HT, m + 1) for m, unit in enumerate(UP_UNITS)}
            read_signal |= {unit: (-2, y_ready, KT, Y_START + m + 1) for m, unit in enumerate(DOWN_UNITS)}

            held = {}

            def dense_bank(st, unit):
                bank = bank_number(st, unit)
                if st.looped:
                    i, before = (st.i, unit - 2) if unit >= 2 else (st.i - 1, unit - 2 + len(read_signal))
                    ahead, signal, per_batch, within = read_signal[before]
                    pe.wait_ge(signal, per_batch * (i + ahead) + within)
                    held[bank] = unit, LOOP_TO - 1 + read_signal[unit][0]
                else:
                    if bank in held:
                        before, batch = held[bank]
                        ahead, signal, per_batch, within = read_signal[before]
                        pe.wait_ge(signal, per_batch * batch + within)
                    elif bank >= 2:
                        pe.wait_ge(maxed, CHUNKS * B)
                    held[bank] = unit, st.i + read_signal[unit][0]
                return unit_bank(st, unit)

            def product(out, passes):
                for n, (w, m) in enumerate(passes):
                    last = nc.tensor.matmul(out, w, m, start=(n == 0), stop=(n == len(passes) - 1))
                return last

            def three(w_hi, w_lo, m_hi, m_lo, ks):
                return [pair for k in ks for pair in ((w_hi(k), m_hi(k)), (w_hi(k), m_lo(k)), (w_lo(k), m_hi(k)))]

            def columns(w, first):
                return lambda k: w[:, k, first:first + P]

            def x_variances(group):
                first, count = ROOT_GROUPS[group]
                pe.wait_ge(x_squared, group + 1)
                pe.wait_ge(x_turned, first)
                for n in range(count):
                    product(x_means[first + n], [(mean_w[:, :], x_squares[group][:, k, n * T:(n + 1) * T]) for k in range(KT)]) \
                        .then_inc(x_averaged, 1)

            def stats(st):
                d = dense_bank(st, STAT2)
                pe.wait_ge(square_sums, st.n + 1)
                product(d[:, 0, :], [(mean_w[:, :], norm_sum[:, :])]).then_inc(stats_done, 1)

            def project(st, unit, first_col, done):
                d = dense_bank(st, unit)
                if st.first:
                    pe.wait_ge(w_lo_done[QK_W], 1)
                pe.wait_ge(norm_hi[0], st.a + 1)
                pe.wait_ge(norm_lo[0], st.a + 1)
                h = st.parity
                for m in range(KT):
                    last = product(d[:, m, :], three(columns(attn_hi, first_col + m * P), columns(attn_lo, first_col + m * P),
                                                     lambda k: h_hi[:, h, k, :], lambda k: h_lo[:, h, k, :], range(KT)))
                last.then_inc(done, 1)

            def values(st):
                d = dense_bank(st, VV)
                h = 1 - st.parity
                for t in range(TT):
                    tok = slice(t * P, t * P + P)
                    last = product(d[:, t, :], three(lambda k: h_hi[:, h, k, tok], lambda k: h_lo[:, h, k, tok],
                                                     lambda k: attn_hi[:, k, 2 * D:3 * D], lambda k: attn_lo[:, k, 2 * D:3 * D],
                                                     range(KT)))
                last.then_inc(v_done, 1)

            def scores(st, chunk):
                g, half = chunk // 2, chunk % 2
                if half == 0:
                    pe.wait_ge(stack_loaded[g], stacked(st, st.s, g))
                if not st.at(-1):
                    pe.wait_ge(maxed, CHUNKS * st.s + chunk)
                elif chunk >= 2:
                    pe.wait_ge(maxed, chunk - 1)
                bank = score_bank(st, chunk)
                buf = stack[1 - st.parity]
                for sl in range(2):
                    for par in range(2):
                        win = slice(64 * par, 64 * par + 64)
                        last = product(bank[:, par, sl, :], [(buf[win, 2 * g + sl, 0, half * P:half * P + P],
                                                              buf[win, 2 * g + sl, 1, :])])
                last.then_inc(scores_done, 1)

            def scores_t(st, chunk):
                g, half = chunk // 2, chunk % 2
                if chunk == 0:
                    pe.wait_ge(m_loaded, 16 * (st.c + 1))
                pe.wait_ge(exp_done, CHUNKS * st.c + chunk)
                buf = stack[st.parity]
                for sl in range(2):
                    for par in range(2):
                        win = slice(64 * par, 64 * par + 64)
                        last = product(st_ps[:, par, sl, :], [(buf[win, 2 * g + sl, 1, half * P:half * P + P],
                                                               buf[win, 2 * g + sl, 0, :])])
                last.then_inc(scores_t_done, 1)

            def probs_v(st, chunk):
                g, half = chunk // 2, chunk % 2
                if chunk == 0:
                    pe.wait_ge(v_ready, 2 * (st.c + 1))
                if chunk == 0 and (st.looped or st.c > 0):
                    pe.wait_ge(o_packed, 4 * st.c - 2)
                if chunk == CHUNKS // 2:
                    pe.wait_ge(o_packed, 4 * st.c)
                pe.wait_ge(exp_done, CHUNKS * st.c + chunk + 1)
                for j in range(4):
                    last = nc.tensor.matmul(o_ps[32 * j:32 * j + 32, g // 2, g % 2, :],
                                            v_aug[st.parity][:, half, g % 2, 4 * (g // 2) + j, :],
                                            probs[:, chunk % 2, j % 2, j // 2, :], start=(half == 0), stop=(half == 1))
                last.then_inc(pv_done, 1)

            def max_rows(st):
                d = dense_bank(st, MT)
                pe.wait_ge(m_split_ready, st.s + 1)
                for t in range(TT):
                    lhs = m_split[:, t, :, :, :].rearrange("p a b s -> p (a b s)").bitcast(F32)
                    last = product(d[0:32, 0, t * P:t * P + P], [(lhs, ident)])
                last.then_inc(m_turned, 1)

            def out_proj(st):
                d = dense_bank(st, WO)
                pe.wait_ge(on_hi_ready, 2 * (st.n + 1))
                pe.wait_ge(on_lo_ready, 2 * (st.n + 1))
                for m in range(KT):
                    last = product(d[:, m, :], three(columns(attn_hi, 3 * D + m * P), columns(attn_lo, 3 * D + m * P),
                                                     lambda k: on_hi[:, k, :], lambda k: on_lo[:, k, :], range(2)))
                last.then_inc(wo_done, 1)

            def ffn_up(st, m):
                d = dense_bank(st, UP_UNITS[m])
                if m == 0:
                    pe.wait_ge(norm_hi[1], st.n + 1)
                    pe.wait_ge(norm_lo[1], st.n + 1)
                for half, (hi, lo) in enumerate(((gate_hi, gate_lo), (hid_hi, hid_lo))):
                    last = product(d[:, half, :], three(columns(hi, m * P), columns(lo, m * P),
                                                        lambda k: g_hi[:, k, :], lambda k: g_lo[:, k, :], range(KT)))
                last.then_inc(f1_done, 1)

            def ffn_down(st, m, half):
                if half == 0:
                    dense_bank(st, DOWN_UNITS[m])
                pe.wait_ge(act_hi_ready, HT * st.f + 4 * (half + 1))
                pe.wait_ge(act_lo_ready, HT * st.f + 4 * (half + 1))
                passes = three(columns(out_hi, m * P), columns(out_lo, m * P),
                               lambda k: act_hi[:, k, :], lambda k: act_lo[:, k, :], range(4 * half, 4 * half + 4))
                for n, (w, mov) in enumerate(passes):
                    last = nc.tensor.matmul(unit_bank(st, DOWN_UNITS[m])[:, m, :], w, mov, start=(half == 0 and n == 0),
                                            stop=(half == 1 and n == len(passes) - 1))
                if half == 1:
                    last.then_inc(f2_done, 1)

            pe.wait_ge(filled, FILLS)
            x_variances(0)

            pe.wait_ge(cond_loaded, 16 * 3)
            for n in range(4 * KT):
                last = product(s_ps[:, 0, 0, n * B:n * B + B], [(cw_sb[:, n // KT, (n % KT) * P:(n % KT) * P + P], ct_sb[:, :])])
            last.then_inc(gb_product, 1)
            pe.wait_ge(const_loaded, 16)

            def fill(st):
                if st.s is not None:
                    pe.wait_ge(w_lo_done[VO_W], 1)
                    values(st)
                    pe.wait_ge(gb_ready, 1)
                    pe.wait_ge(score_rows_loaded, 64)
                    scores(st, 0)
                    scores(st, 1)
                if st.c is not None:
                    pe.wait_ge(x_turned, B)
                    scores_t(st, 0)
                project(st, QQ, 0, q_done)
                if st.c is not None:
                    scores_t(st, 1)
                if st.s is not None:
                    scores(st, 2)
                if st.c is not None:
                    probs_v(st, 0)
                    scores_t(st, 2)
                    probs_v(st, 1)
                if st.s is not None:
                    scores(st, 3)
                if st.c is not None:
                    scores_t(st, 3)
                project(st, KK, D, k_done)
                if st.c is not None:
                    probs_v(st, 2)
                    scores_t(st, 4)
                if st.s is not None:
                    scores(st, 4)
                if st.c is not None:
                    probs_v(st, 3)
                    scores_t(st, 5)
                if st.s is not None:
                    scores(st, 5)
                if st.at(-1):
                    x_variances(2)
                if st.c is not None:
                    probs_v(st, 4)
                    scores_t(st, 6)
                if st.s is not None:
                    scores(st, 6)
                if st.first:
                    x_variances(1)
                if st.c is not None:
                    scores_t(st, 7)
                    probs_v(st, 5)
                if st.s is not None:
                    scores(st, 7)
                if st.c is not None:
                    probs_v(st, 6)
                    probs_v(st, 7)
                if st.s is not None:
                    max_rows(st)

            def steady(st):
                if st.at(1):
                    for w in (GATE, HID, OUT):
                        pe.wait_ge(w_lo_done[w], 1)
                scores(st, 0)
                values(st)
                if st.f is not None:
                    ffn_up(st, 4)
                    ffn_up(st, 5)
                scores_t(st, 0)
                if st.f is not None:
                    ffn_up(st, 6)
                scores(st, 1)
                scores_t(st, 1)
                probs_v(st, 0)
                out_proj(st)
                scores_t(st, 2)
                if st.f is not None:
                    ffn_up(st, 7)
                scores(st, 2)
                probs_v(st, 1)
                probs_v(st, 2)
                scores_t(st, 3)
                scores(st, 3)
                stats(st)
                if st.a is not None:
                    project(st, QQ, 0, q_done)
                probs_v(st, 3)
                scores(st, 4)
                if st.a is not None:
                    project(st, KK, D, k_done)
                scores_t(st, 4)
                if st.f is not None:
                    ffn_down(st, 0, 0)
                    ffn_down(st, 0, 1)
                scores(st, 5)
                scores_t(st, 5)
                if st.f is not None:
                    ffn_down(st, 1, 0)
                    ffn_down(st, 1, 1)
                probs_v(st, 4)
                probs_v(st, 5)
                scores_t(st, 6)
                scores(st, 6)
                ffn_up(st, 0)
                ffn_up(st, 1)
                scores_t(st, 7)
                scores(st, 7)
                ffn_up(st, 2)
                ffn_up(st, 3)
                probs_v(st, 6)
                probs_v(st, 7)
                max_rows(st)

            def drain(st):
                ffn_up(st, 4)
                ffn_up(st, 5)
                if st.c is not None:
                    scores_t(st, 0)
                ffn_up(st, 6)
                if st.c is not None:
                    scores_t(st, 1)
                    probs_v(st, 0)
                if st.n is not None:
                    out_proj(st)
                ffn_up(st, 7)
                if st.c is not None:
                    scores_t(st, 2)
                    probs_v(st, 1)
                    scores_t(st, 3)
                    probs_v(st, 2)
                if st.n is not None:
                    stats(st)
                if st.c is not None:
                    probs_v(st, 3)
                    scores_t(st, 4)
                ffn_down(st, 0, 0)
                if st.f == B - 1:
                    ffn_down(st, 1, 0)
                ffn_down(st, 0, 1)
                if st.c is not None:
                    scores_t(st, 5)
                    probs_v(st, 4)
                    scores_t(st, 6)
                if st.f < B - 1:
                    ffn_down(st, 1, 0)
                ffn_down(st, 1, 1)
                if st.c is not None:
                    probs_v(st, 5)
                    probs_v(st, 6)
                    scores_t(st, 7)
                if st.n is not None:
                    ffn_up(st, 0)
                    ffn_up(st, 1)
                if st.c is not None:
                    probs_v(st, 7)
                if st.n is not None:
                    ffn_up(st, 2)
                    ffn_up(st, 3)

            steps(pe, fill, steady, drain)

        @block.scalar
        def _(act):

            def split_hi(w):
                act.wait_ge(w_loaded[w], 16)
                nc.scalar.activation(w_hi_sb[w], w_raw[w], ACT.Copy).then_inc(w_hi_done[w], 1)

            def norm_round(st, n, b):
                dst = h_hi[:, st.parity, :, :] if n == 0 else g_hi[:, :, :]
                act.wait_ge(norm_ready[n], 2 * (b + 1))
                norm_buffer_free(act, st, n)
                nc.scalar.activation(dst, norm_y[n][:, :, :], ACT.Copy).then_inc(norm_hi[n], 1)

            def exps(st, chunk):
                act.wait_ge(scores_t_done, CHUNKS * st.c + chunk + 1)
                if chunk >= 2 or st.looped or st.c > 0:
                    act.wait_ge(pv_done, CHUNKS * st.c + chunk - 1)
                nc.scalar.activation(probs[:, chunk % 2, :, :, :], st_ps[:, :, :, :], ACT.Exp).then_inc(exp_done, 1)

            def square_x(group):
                first, count = ROOT_GROUPS[group]
                act.wait_ge(x_loaded[group], 16)
                if group == 1:
                    act.wait_ge(gb_product, 1)
                if group == 2:
                    act.wait_ge(x_averaged, first)
                nc.scalar.activation(x_squares[group], x_sb[:, :, first * T:(first + count) * T], ACT.Square).then_inc(x_squared, 1)

            def tanh(st, m):
                b = st.n if m < HT // 2 else st.f
                act.wait_ge(f1_done, HT * b + m + 1)
                if m >= 2 or st.looped or b > 0:
                    act.wait_ge(act_ready, HT * b + m - 1)
                nc.scalar.activation(th[:, m % 2, :], unit_bank(st, UP_UNITS[m])[:, 0, :], ACT.Tanh, scale=0.5).then_inc(tanh_ready, 1)

            def act_round(st, m):
                act.wait_ge(act_ready, HT * (st.n if m < HT // 2 - 1 else st.f) + m + 1)
                nc.scalar.activation(act_hi[:, m, :], act_f[:, m % 4, :], ACT.Copy).then_inc(act_hi_ready, 1)

            def o_parts(b, pair):
                act.wait_ge(pv_done, CHUNKS * b + 4 * (pair + 1))
                if not isinstance(b, int) or b > 0:
                    act.wait_ge(o_normed, 2 * b + pair - 1)
                nc.scalar.activation(o_part[:, pair, :], o_ps[:, pair, 0, :], ACT.Identity, scale=rows_lo).then_inc(o_parts_ready, 1)
                nc.scalar.activation(s_part[:, pair, :], o_ps[:, pair, 0, :], ACT.Identity, scale=rows_hi).then_inc(o_parts_ready, 1)

            def q_round(st):
                if not st.first:
                    for g in range(GROUPS):
                        act.wait_ge(stack_loaded[g], stacked(st, st.a - 1, g))
                act.wait_ge(q_done, st.a + 1)
                nc.scalar.activation(qk[:, :, Q_HI, :], unit_bank(st, QQ)[:, :, :], ACT.Copy, scale=QSCALE).then_inc(qk_hi_ready, 1)

            def k_round(st):
                act.wait_ge(k_done, st.a + 1)
                nc.scalar.activation(qk[:, :, K_HI, :], unit_bank(st, KK)[:, :, :], ACT.Copy).then_inc(qk_hi_ready, 1)

            def o_round(b, pair):
                act.wait_ge(o_normed, 2 * b + pair + 1)
                act.wait_ge(wo_done, b)
                nc.scalar.activation(on_hi[:, pair, :], o_norm[:, pair, :], ACT.Copy).then_inc(on_hi_ready, 1)

            def square_x1(st):
                act.wait_ge(x1_ready, st.n + 1)
                act.wait_ge(norm_hi[1], st.n)
                act.wait_ge(norm_lo[1], st.n)
                nc.scalar.activation(norm_sq[1][:, :, :], x1[:, :, :], ACT.Square).then_inc(squares, 1)

            def place_v(st):
                act.wait_ge(v_done, st.s + 1)
                if st.looped or st.s >= 2:
                    act.wait_ge(pv_done, CHUNKS * (st.s - 1))
                for e in range(2):
                    src = unit_bank(st, VV)[:, :, P * e:P * e + P].rearrange("p t (s d) -> p t s d", d=DH)
                    dst = v_aug[1 - st.parity][:, :, e, :, DH * e:DH * e + DH]
                    nc.scalar.activation(dst, src, ACT.Copy).then_inc(v_ready, 1)

            square_x(0)
            split_hi(QK_W)
            act.wait_ge(const_loaded, 16)
            act.wait_ge(filled, FILLS)

            def fill(st):
                if st.s is not None:
                    place_v(st)
                norm_round(st, 0, st.a)
                if st.first:
                    square_x(1)
                    split_hi(VO_W)
                if st.at(-1):
                    split_hi(HID)
                if st.c is not None:
                    exps(st, 0)
                    exps(st, 1)
                    exps(st, 2)
                    exps(st, 3)
                q_round(st)
                k_round(st)
                if st.c is not None:
                    exps(st, 4)
                    for w in range(5):
                        act.wait_ge(w_lo_done[w], 1)
                    o_parts(st.c, 0)
                if st.at(-1):
                    split_hi(OUT)
                if st.c is not None:
                    exps(st, 5)
                    exps(st, 6)
                    exps(st, 7)
                    o_parts(st.c, 1)
                    o_round(st.c, 0)
                if st.first:
                    split_hi(GATE)
                    square_x(2)

            def steady(st):
                place_v(st)
                if st.f is not None:
                    tanh(st, 4)
                    act_round(st, 3)
                    tanh(st, 5)
                exps(st, 0)
                if st.f is not None:
                    act_round(st, 4)
                o_round(st.n, 1)
                if st.f is not None:
                    tanh(st, 6)
                    act_round(st, 5)
                exps(st, 1)
                if st.a is not None:
                    norm_round(st, 0, st.a)
                exps(st, 2)
                square_x1(st)
                if st.f is not None:
                    tanh(st, 7)
                exps(st, 3)
                if st.f is not None:
                    act_round(st, 6)
                    act_round(st, 7)
                if st.a is not None:
                    q_round(st)
                o_parts(st.c, 0)
                if st.a is not None:
                    k_round(st)
                exps(st, 4)
                exps(st, 5)
                norm_round(st, 1, st.n)
                exps(st, 6)
                tanh(st, 0)
                tanh(st, 1)
                act_round(st, 0)
                exps(st, 7)
                o_round(st.c, 0)
                tanh(st, 2)
                tanh(st, 3)
                o_parts(st.c, 1)
                act_round(st, 1)
                act_round(st, 2)

            def drain(st):
                tanh(st, 4)
                tanh(st, 5)
                if st.c is not None:
                    exps(st, 0)
                if st.n is not None:
                    o_round(st.n, 1)
                act_round(st, 3)
                if st.c is not None:
                    exps(st, 1)
                tanh(st, 6)
                act_round(st, 4)
                act_round(st, 5)
                if st.c is not None:
                    exps(st, 2)
                if st.n is not None:
                    square_x1(st)
                tanh(st, 7)
                if st.c is not None:
                    exps(st, 3)
                act_round(st, 6)
                act_round(st, 7)
                if st.c is not None:
                    o_parts(st.c, 0)
                    exps(st, 4)
                    exps(st, 5)
                    exps(st, 6)
                if st.n is not None:
                    norm_round(st, 1, st.n)
                if st.c is not None:
                    exps(st, 7)
                if st.n is not None:
                    tanh(st, 0)
                    tanh(st, 1)
                if st.c is not None:
                    o_parts(st.c, 1)
                if st.n is not None:
                    act_round(st, 0)
                    tanh(st, 2)
                    act_round(st, 1)
                    tanh(st, 3)
                    act_round(st, 2)
                if st.c is not None:
                    o_round(st.c, 0)

            steps(act, fill, steady, drain)

        @block.vector
        def _(dve):
            def split_lo(w):
                dve.wait_ge(w_hi_done[w], 1)
                nc.vector.tensor_tensor(w_lo_sb[w], w_raw[w], w_hi_sb[w].bitcast(F32),
                                        ALU.subtract).then_inc(w_lo_done[w], 1)

            def first_guess(y, v_half, v, count):
                nc.vector.tensor_scalar(v_half, v, -0.5, None, ALU.mult).then_inc(count, 1)
                nc.vector.tensor_scalar(y.bitcast(I32), v.bitcast(I32), -0.5, RSQRT_MAGIC, ALU.mult, ALU.add).then_inc(count, 1)

            def x_roots(group):
                first, count = ROOT_GROUPS[group]
                done = root_steps(group - 1)
                dve.wait_ge(x_averaged, first + count)
                for b in range(first, first + count):
                    part = slice(b * BLOCKS, (b + 1) * BLOCKS)
                    if b >= 2:
                        dve.wait_ge(root_step, variances_through(b - 2))
                    nc.vector.transpose(turned_x[:, b % 2].rearrange("p a c -> p (a c)"), x_means[b]).then_inc(x_turned, 1)
                    dve.wait_ge(x_turned, b + 1)
                    nc.vector.tensor_scalar(roots[:, 3, part], turned_x[:, b % 2, :, 0], EPS, None, ALU.add).then_inc(root_step, 1)
                dve.wait_ge(root_step, done + count)
                part = slice(first * BLOCKS, (first + count) * BLOCKS)
                first_guess(roots[:, 1, part], roots[:, 0, part], roots[:, 3, part], root_step)

            def stats_turn(st):
                b = st.n
                dve.wait_ge(stats_done, b + 1)
                dve.wait_ge(newton_step, NEWTON_STEPS * b)
                nc.vector.transpose(norm_tr[:, :, :].rearrange("p a c -> p (a c)"), unit_bank(st, STAT2)[:, 0, :]) \
                    .then_inc(stats_turned, 1)
                dve.wait_ge(stats_turned, b + 1)
                nc.vector.tensor_scalar(newton[:, 3, :], norm_tr[:, :, 0], EPS, None, ALU.add).then_inc(newton_step, 1)
                dve.wait_ge(newton_step, NEWTON_STEPS * b + 1)
                first_guess(newton[:, 1, :], newton[:, 0, :], newton[:, 3, :], newton_step)

            def spread_roots(st, n, b):
                if n == 0:
                    dve.wait_ge(root_step, root_steps(group_of(st)))
                    dve.wait_ge(inv_spread[0], b)
                    nc.vector.tensor_copy(x_root[:, :], roots[:, 1, bass.ds(b * BLOCKS, BLOCKS)]).then_inc(root_taken, 1)
                    dve.wait_ge(root_taken, b + 1)
                    root = x_root[:, :]
                else:
                    dve.wait_ge(newton_step, NEWTON_STEPS * (b + 1))
                    root = newton[:, 1, :]
                dve.wait_ge(x_scaled[n], b)
                if n == 0 and (st.looped or b >= 4):
                    dve.wait_ge(x_scaled[1], b - 3)
                if n == 1:
                    dve.wait_ge(x_scaled[0], b + 4 if st.looped or b + 4 <= B else B)
                nc.vector.transpose(norm_inv[:, :], root.unsqueeze(2).broadcast_to([P, BLOCKS, 32])).then_inc(inv_spread[n], 1)

            def normalise(st, n, b):
                spread_roots(st, n, b)
                dve.wait_ge(inv_spread[n], b + 1)
                dve.wait_ge(norm_hi[n], b)
                dve.wait_ge(norm_lo[n], b)
                src = x_sb[:, :, tokens(b)] if n == 0 else x1[:, :, :]
                nc.vector.tensor_tensor(norm_x[n][:, :, :], src, norm_inv[:, :].unsqueeze(1).broadcast_to([P, KT, T]),
                                        ALU.mult).then_inc(x_scaled[n], 1)
                dve.wait_ge(x_scaled[n], b + 1)
                for k in range(KT):
                    scale = gb[:, (2 * n) * KT + k, bass.ds(b, 1)]
                    shift = gb[:, (2 * n + 1) * KT + k, bass.ds(b, 1)]
                    nc.vector.tensor_scalar(norm_y[n][:, k, :], norm_x[n][:, k, :], scale, shift, ALU.mult, ALU.add) \
                        .then_inc(norm_ready[n], 1)

            def maxima(st, chunk):
                bank = score_bank(st, chunk)
                g, half = chunk // 2, chunk % 2
                dve.wait_ge(scores_done, CHUNKS * st.s + chunk + 1)
                nc.vector.tensor_reduce(m_raw[:, half, :, 2 * g:2 * g + 2], bank[:, :, :, :], AX.X, ALU.max).then_inc(maxed, 1)

            def gated(st, m):
                bank = unit_bank(st, UP_UNITS[m])
                b = st.n if m < HT // 2 else st.f
                dve.wait_ge(tanh_ready, HT * b + m + 1)
                nc.vector.scalar_tensor_tensor(th[:, m % 2, :], th[:, m % 2, :], 1.0, bank[:, 0, :], ALU.add, ALU.mult) \
                    .then_inc(silu_ready, 1)
                dve.wait_ge(silu_ready, HT * b + m + 1)
                if m >= 4 or st.looped or b > 0:
                    dve.wait_ge(act_hi_ready, HT * b + m - 3)
                    dve.wait_ge(act_lo_ready, HT * b + m - 3)
                nc.vector.tensor_tensor(act_f[:, m % 4, :], th[:, m % 2, :], bank[:, 1, :], ALU.mult) \
                    .then_inc(act_ready, 1)

            def pack(b, pair):
                dve.wait_ge(o_parts_ready, 4 * b + 2 * pair + 2)
                if not isinstance(b, int) or b > 0:
                    dve.wait_ge(on_hi_ready, 2 * b + pair - 1)
                    dve.wait_ge(on_lo_ready, 2 * b + pair - 1)
                nc.vector.scalar_tensor_tensor(o_pack[:, pair, :], o_ps[:, pair, 1, :], rows_hi, o_part[:, pair, :],
                                               ALU.mult, ALU.add).then_inc(o_packed, 1)
                nc.vector.scalar_tensor_tensor(s_pack[:, pair, :], o_ps[:, pair, 1, :], rows_lo, s_part[:, pair, :],
                                               ALU.mult, ALU.add).then_inc(o_packed, 1)

            def swap_sums(b, pair):
                dve.wait_ge(const_loaded, 16)
                dve.wait_ge(o_packed, 4 * b + 2 * pair + 2)
                nc.vector.stream_shuffle(s_bcast[:, pair, :], s_pack[:, pair, :], [(p + DH) % 32 for p in range(32)]) \
                    .then_inc(s_spread, 1)

            def invert(b, pair):
                dve.wait_ge(s_spread, 2 * b + pair + 1)
                nc.vector.reciprocal(s_recip[:, pair, :], s_bcast[:, pair, :]).then_inc(s_inverted, 1)

            def divide(b, pair):
                dve.wait_ge(s_inverted, 2 * b + pair + 1)
                nc.vector.tensor_tensor(o_norm[:, pair, :], o_pack[:, pair, :], s_recip[:, pair, :], ALU.mult) \
                    .then_inc(o_normed, 1)

            def q_rest(st):
                dve.wait_ge(qk_hi_ready, 2 * st.a + 1)
                nc.vector.scalar_tensor_tensor(qk[:, :, Q_LO, :], unit_bank(st, QQ)[:, :, :], QSCALE,
                                               qk[:, :, Q_HI, :].bitcast(F32), ALU.mult, ALU.subtract).then_inc(qk_lo_ready, 1)

            def k_rest(st):
                dve.wait_ge(qk_hi_ready, 2 * st.a + 2)
                nc.vector.tensor_tensor(qk[:, :, K_LO, :], unit_bank(st, KK)[:, :, :], qk[:, :, K_HI, :].bitcast(F32),
                                        ALU.subtract).then_inc(qk_lo_ready, 1)

            def add_x(st):
                dve.wait_ge(wo_done, st.n + 1)
                dve.wait_ge(squares, st.n)
                dve.wait_ge(resid_ready, st.n)
                nc.vector.tensor_tensor(x1[:, :, :], unit_bank(st, WO)[:, :, :], x_sb[:, :, tokens(st.n)], ALU.add).then_inc(x1_ready, 1)

            def split_maxima(st):
                dve.wait_ge(maxed, CHUNKS * (st.s + 1))
                dve.wait_ge(m_turned, st.s)
                nc.vector.tensor_copy(m_split[:, :, :, 0, :], m_raw[:, :, :, :]).then_inc(m_hi_ready, 1)
                dve.wait_ge(m_hi_ready, st.s + 1)
                nc.vector.tensor_tensor(m_split[:, :, :, 1, :], m_raw[:, :, :, :], m_split[:, :, :, 0, :].bitcast(F32),
                                        ALU.subtract).then_inc(m_split_ready, 1)

            def take_max_rows(st):
                dve.wait_ge(m_turned, st.s + 1)
                dve.wait_ge(m_loaded, 16 * st.s)
                nc.vector.tensor_copy(m_rows[:, :], unit_bank(st, MT)[0:32, 0, :]).then_inc(m_rows_ready, 1)

            def result(st, m):
                dve.wait_ge(f2_done, 2 * st.f + m + 1)
                dve.wait_ge(resid_ready, st.f + 1)
                dve.wait_ge(y_stored, STORE_START + 16 * st.f)
                nc.vector.scalar_tensor_tensor(y_sb[:, m, :], unit_bank(st, DOWN_UNITS[m])[:, m, :], 0.5, resid[:, st.parity, m, :],
                                               ALU.mult, ALU.add).then_inc(y_ready, 1)

            nc.vector.memset(mean_w[:, :], 1.0 / D).then_inc(filled, 1)
            nc.vector.memset(zero_rows[:, :], 0.0).then_inc(filled, 1)
            x_roots(0)
            split_lo(QK_W)
            dve.wait_ge(gb_product, 1)
            dve.wait_ge(cond_loaded, 16 * 3)
            nc.vector.tensor_tensor(gb[:, :, :], s_ps[:, 0, 0, 0:4 * KT * B].rearrange("p (a b) -> p a b", b=B),
                                    cb_sb[:, :].unsqueeze(2).broadcast_to([P, 4 * KT, B]), ALU.add).then_inc(gb_ready, 1)
            dve.wait_ge(gb_ready, 1)
            dve.wait_ge(x_loaded[0], 16)
            dve.wait_ge(const_loaded, 16)

            def fill(st):
                if st.at(-1):
                    dve.wait_ge(x_loaded[1], 16)
                normalise(st, 0, st.a)
                if st.s is not None:
                    maxima(st, 0)
                    maxima(st, 1)
                    maxima(st, 2)
                    maxima(st, 3)
                q_rest(st)
                k_rest(st)
                if st.first:
                    x_roots(1)
                if st.s is not None:
                    maxima(st, 4)
                if st.c is not None:
                    pack(st.c, 0)
                if st.s is not None:
                    maxima(st, 5)
                if st.c is not None:
                    swap_sums(st.c, 0)
                if st.s is not None:
                    maxima(st, 6)
                if st.c is not None:
                    invert(st.c, 0)
                if st.s is not None:
                    maxima(st, 7)
                    split_maxima(st)
                if st.c is not None:
                    pack(st.c, 1)
                if st.first:
                    split_lo(VO_W)
                if st.s is not None:
                    take_max_rows(st)
                if st.at(-1):
                    x_roots(2)
                if st.c is not None:
                    swap_sums(st.c, 1)
                if st.first:
                    split_lo(GATE)
                if st.c is not None:
                    divide(st.c, 0)
                    invert(st.c, 1)

            def steady(st):
                if st.at(1):
                    dve.wait_ge(x_loaded[2], 16)
                if st.f is not None:
                    gated(st, 4)
                maxima(st, 0)
                divide(st.n, 1)
                if st.f is not None:
                    gated(st, 5)
                    gated(st, 6)
                if st.a is not None:
                    normalise(st, 0, st.a)
                maxima(st, 1)
                add_x(st)
                maxima(st, 2)
                if st.f is not None:
                    gated(st, 7)
                maxima(st, 3)
                stats_turn(st)
                if st.a is not None:
                    q_rest(st)
                maxima(st, 4)
                pack(st.c, 0)
                if st.a is not None:
                    k_rest(st)
                normalise(st, 1, st.n)
                swap_sums(st.c, 0)
                maxima(st, 5)
                if st.f is not None:
                    result(st, 0)
                    result(st, 1)
                invert(st.c, 0)
                maxima(st, 6)
                gated(st, 0)
                divide(st.c, 0)
                gated(st, 1)
                maxima(st, 7)
                gated(st, 2)
                split_maxima(st)
                gated(st, 3)
                take_max_rows(st)
                pack(st.c, 1)
                swap_sums(st.c, 1)
                invert(st.c, 1)

            def drain(st):
                if st.n is not None:
                    divide(st.n, 1)
                gated(st, 4)
                gated(st, 5)
                gated(st, 6)
                if st.n is not None:
                    add_x(st)
                gated(st, 7)
                if st.n is not None:
                    stats_turn(st)
                result(st, 0)
                if st.c is not None:
                    pack(st.c, 0)
                if st.n is not None:
                    normalise(st, 1, st.n)
                if st.c is not None:
                    swap_sums(st.c, 0)
                    invert(st.c, 0)
                    divide(st.c, 0)
                result(st, 1)
                if st.n is not None:
                    gated(st, 0)
                    gated(st, 1)
                if st.c is not None:
                    pack(st.c, 1)
                    swap_sums(st.c, 1)
                if st.n is not None:
                    gated(st, 2)
                if st.c is not None:
                    invert(st.c, 1)
                if st.n is not None:
                    gated(st, 3)

            steps(dve, fill, steady, drain)

        @block.gpsimd
        def _(pool):
            for n in range(2):
                nc.gpsimd.memset(v_aug[n][:, :, :, :, :], 1.0).then_inc(filled, 1)
            nc.gpsimd.memset(three_halves[:, :], 1.5).then_inc(filled, 1)
            pool.wait_ge(filled, FILLS)

            def newtons(y, v_half, w, count, done):
                for _ in range(NEWTONS):
                    for op in (lambda: nc.gpsimd.tensor_tensor(w, y, y, ALU.mult),
                               lambda: nc.gpsimd.tensor_tensor(w, w, v_half, ALU.mult),
                               lambda: nc.gpsimd.tensor_tensor(w, w, three_halves[:, 0:w.shape[-1]], ALU.add),
                               lambda: nc.gpsimd.tensor_tensor(y, y, w, ALU.mult)):
                        pool.wait_ge(count, done)
                        op().then_inc(count, 1)
                        done += 1

            def x_newtons(group):
                first, count = ROOT_GROUPS[group]
                part = slice(first * BLOCKS, (first + count) * BLOCKS)
                newtons(roots[:, 1, part], roots[:, 0, part], roots[:, 2, part], root_step, root_steps(group) - 4 * NEWTONS)

            def split_lo(w):
                pool.wait_ge(w_hi_done[w], 1)
                nc.gpsimd.tensor_tensor(w_lo_sb[w], w_raw[w], w_hi_sb[w].bitcast(F32), ALU.subtract).then_inc(w_lo_done[w], 1)

            def add_squares(st):
                pool.wait_ge(squares, st.n + 1)
                pool.wait_ge(stats_done, st.n)
                nc.gpsimd.tensor_tensor(norm_sum[:, :], norm_sq[1][:, 0, :], norm_sq[1][:, 1, :], ALU.add) \
                    .then_inc(square_sums, 1)

            def norm_rest(st, n, b):
                hi, lo = (h_hi[:, st.parity], h_lo[:, st.parity]) if n == 0 else (g_hi, g_lo)
                pool.wait_ge(norm_hi[n], b + 1)
                norm_buffer_free(pool, st, n)
                nc.gpsimd.tensor_tensor(lo[:, :, :], norm_y[n][:, :, :], hi[:, :, :].bitcast(F32), ALU.subtract) \
                    .then_inc(norm_lo[n], 1)

            def act_rest(st, m):
                pool.wait_ge(act_hi_ready, HT * (st.n if m < HT // 2 - 1 else st.f) + m + 1)
                nc.gpsimd.tensor_tensor(act_lo[:, m, :], act_f[:, m % 4, :], act_hi[:, m, :].bitcast(F32), ALU.subtract) \
                    .then_inc(act_lo_ready, 1)

            def o_rest(b, pair):
                pool.wait_ge(on_hi_ready, 2 * b + pair + 1)
                pool.wait_ge(wo_done, b)
                nc.gpsimd.tensor_tensor(on_lo[:, pair, :], o_norm[:, pair, :], on_hi[:, pair, :].bitcast(F32), ALU.subtract) \
                    .then_inc(on_lo_ready, 1)

            def residual(st):
                pool.wait_ge(x1_ready, st.n + 1)
                if st.looped or st.n >= 2:
                    pool.wait_ge(y_ready, Y_START + 2 * (st.n - 1))
                nc.gpsimd.tensor_tensor(resid[:, 1 - st.parity, :, :], x1[:, :, :], x_sb[:, :, tokens(st.n)], ALU.add) \
                    .then_inc(resid_ready, 1)

            x_newtons(0)

            def fill(st):
                norm_rest(st, 0, st.a)
                if st.at(-1):
                    split_lo(HID)
                if st.first:
                    x_newtons(1)
                if st.at(-1):
                    split_lo(OUT)
                    x_newtons(2)
                if st.c is not None:
                    o_rest(st.c, 0)

            def steady(st):
                if st.at(1):
                    for n in range(3):
                        pool.wait_ge(x_loaded[n], 16)
                if st.f is not None:
                    act_rest(st, 3)
                o_rest(st.n, 1)
                if st.f is not None:
                    act_rest(st, 4)
                if st.a is not None:
                    norm_rest(st, 0, st.a)
                if st.f is not None:
                    act_rest(st, 5)
                add_squares(st)
                if st.f is not None:
                    act_rest(st, 6)
                    act_rest(st, 7)
                newtons(newton[:, 1, :], newton[:, 0, :], newton[:, 2, :], newton_step, NEWTON_STEPS * st.n + 3)
                residual(st)
                norm_rest(st, 1, st.n)
                o_rest(st.c, 0)
                act_rest(st, 0)
                act_rest(st, 1)
                act_rest(st, 2)

            def drain(st):
                if st.n is not None:
                    o_rest(st.n, 1)
                act_rest(st, 3)
                act_rest(st, 4)
                act_rest(st, 5)
                if st.n is not None:
                    add_squares(st)
                act_rest(st, 6)
                act_rest(st, 7)
                if st.n is not None:
                    newtons(newton[:, 1, :], newton[:, 0, :], newton[:, 2, :], newton_step, NEWTON_STEPS * st.n + 3)
                    residual(st)
                    norm_rest(st, 1, st.n)
                    act_rest(st, 0)
                if st.c is not None:
                    o_rest(st.c, 0)
                if st.n is not None:
                    act_rest(st, 1)
                    act_rest(st, 2)

            steps(pool, fill, steady, drain)


def kernel(x, cond_256, L0_cond_Wq, L0_cond_Wk, L0_cond_Wv, L0_cond_Wo, L0_cond_g1w, L0_cond_g1b, L0_cond_b1w, L0_cond_b1b,
           L0_cond_g2w, L0_cond_g2b, L0_cond_b2w, L0_cond_b2b, L0_cond_gate_w, L0_cond_hid_w, L0_cond_out_w):
    import numpy as np
    import concourse.bacc as bacc
    from concourse.bass_utils import run_bass_kernel_spmd

    def contraction_major(w_t, tiles):
        return np.ascontiguousarray(w_t.reshape(tiles, P, -1).transpose(1, 0, 2))

    w = {k: np.asarray(v) for k, v in dict(q=L0_cond_Wq, k=L0_cond_Wk, v=L0_cond_Wv, o=L0_cond_Wo).items()}
    wv = w["v"].T.reshape(D, 2, 2, 4, DH).transpose(0, 2, 1, 3, 4).reshape(D, D)
    wo = w["o"].T.reshape(2, 2, 4, DH, D).transpose(0, 2, 1, 3, 4).reshape(D, D)
    attn = contraction_major(np.concatenate([w["q"].T, w["k"].T, wv, wo], axis=1), KT)
    conds = [np.asarray(v) for v in (L0_cond_g1w, L0_cond_b1w, L0_cond_g2w, L0_cond_b2w)]
    biases = [np.asarray(v).reshape(KT, P) for v in (L0_cond_g1b, L0_cond_b1b, L0_cond_g2b, L0_cond_b2b)]
    rows = np.arange(P) % 32 < DH
    consts = np.concatenate([np.eye(P, dtype=np.float32), rows[:, None].astype(np.float32), (~rows)[:, None].astype(np.float32)], axis=1)
    score_rows = np.zeros((32, SLOTS, T), np.float32)
    for n in range(32):
        score_rows[n, n % SLOTS, :] = -1.0
    arrays = {
        "x_t": np.ascontiguousarray(np.asarray(x).reshape(B * T, KT, P).transpose(2, 1, 0)),
        "cond_t": np.ascontiguousarray(np.asarray(cond_256).T),
        "cond_w": np.ascontiguousarray(np.stack([c.T for c in conds], axis=1)),
        "cond_b": np.ascontiguousarray(np.concatenate(biases, axis=0).T),
        "w_attn": attn,
        "w_gate": contraction_major(np.asarray(L0_cond_gate_w).T, KT).reshape(P, -1),
        "w_hid": contraction_major(np.asarray(L0_cond_hid_w).T, KT).reshape(P, -1),
        "w_out": contraction_major(np.asarray(L0_cond_out_w).T, HT).reshape(P, -1),
        "consts": consts,
        "score_rows": score_rows,
    }
    nc = bacc.Bacc("TRN2", target_bir_lowering=False, num_devices=1)
    args = [nc.dram_tensor(name, a.shape, mybir.dt.from_np(a.dtype), kind="ExternalInput").ap() for name, a in arrays.items()]
    out = nc.dram_tensor("out_t", (P, KT, B * T), F32, kind="ExternalOutput").ap()
    layer_kernel(nc, *args, out)
    r = run_bass_kernel_spmd(nc, [arrays], core_ids=[0])
    y = r.results[0]["out_t"]
    return y.transpose(2, 1, 0).reshape(B, T, D)
```
